# Optimizing a Trainium2 kernel written in Bass

```python
import numpy as np
import jax
import jax.numpy as jnp

def _softmax(x, axis=-1):
    return jax.nn.softmax(x, axis=axis)

def _gelu(x):
    return jax.nn.gelu(x, approximate=True)

def _silu(x):
    return jax.nn.silu(x)

def _sigmoid(x):
    return jax.nn.sigmoid(x)

def _layernorm(x, axis=-1, eps=1e-05):
    m = jnp.mean(x, axis=axis, keepdims=True)
    v = jnp.var(x, axis=axis, keepdims=True)
    return (x - m) / jnp.sqrt(v + eps)

def _scatter_add(tgt, idx, src, axis=0):
    return tgt.at[idx].add(src)

def _segment_sum(src, seg, n):
    return jax.ops.segment_sum(src, seg, n)
kernel_name = 'mk_vit_tower_d1_tok_img1024_r4_f1b3a9'

def setup_inputs(seed: int=0):
    np.random.seed(seed)
    _w = jnp.asarray

    def _rec_inputs():
        import jax
        import jax.numpy as jnp
        _rk = jax.random.key(seed)
        x = -0.00016672 + 0.999947 * jax.random.normal(jax.random.fold_in(_rk, 1), (32, 3, 96, 96), jnp.float32)
        return x
    x = _rec_inputs()

    def _L0_tok_setup():
        import jax, jax.numpy as jnp
        import numpy as np
        P = 16

        def _patchify(x):
            B, C, H, W = x.shape
            gh, gw = (H // P, W // P)
            x = x.reshape(B, C, gh, P, gw, P)
            x = x.transpose(0, 2, 4, 1, 3, 5)
            return x.reshape(B, gh * gw, C * P * P)
        key = jax.random.key(seed)
        k1, k2, k3, k4, k5 = jax.random.split(key, 5)
        B, C, S = (64, 3, 96)
        lin_in, lout = (P * P * C, 256)
        n_patches = (S // P) ** 2
        return {'x': jax.random.normal(k1, (B, C, S, S), dtype=jnp.float32), 'W': jax.random.normal(k2, (lout, lin_in), dtype=jnp.float32) * 0.02, 'b': jax.random.normal(k3, (lout,), dtype=jnp.float32) * 0.02, 'class_token': jax.random.normal(k4, (1, 1, lout), dtype=jnp.float32) * 0.02, 'pos_embedding': jax.random.normal(k5, (1, n_patches + 1, lout), dtype=jnp.float32) * 0.02}
    _L0_tok_all = _L0_tok_setup()
    _L0_tok_in = {k: v for k, v in _L0_tok_all.items() if k in ('W', 'b', 'class_token', 'pos_embedding')}
    del _L0_tok_all

    def _L0_attn_setup():
        import jax, jax.numpy as jnp
        import numpy as np
        EPS = 1e-05

        def layer_norm(x, w, b):
            mu = jnp.mean(x, axis=-1, keepdims=True)
            var = jnp.var(x, axis=-1, keepdims=True)
            return (x - mu) / jnp.sqrt(var + EPS) * w + b
        key = jax.random.key(seed)
        B, N, C = (4, 1024, 256)
        H = 16
        MW = 4 * C
        ks = jax.random.split(key, 8)
        s = 0.02
        return {'x': jax.random.normal(ks[0], (B, N, C), dtype=jnp.float32), 'ln1_w': jnp.ones((C,), jnp.float32), 'ln1_b': jnp.zeros((C,), jnp.float32), 'q_w': jax.random.normal(ks[1], (C, C), jnp.float32) * s, 'q_b': jnp.zeros((C,), jnp.float32), 'k_w': jax.random.normal(ks[2], (C, C), jnp.float32) * s, 'k_b': jnp.zeros((C,), jnp.float32), 'v_w': jax.random.normal(ks[3], (C, C), jnp.float32) * s, 'v_b': jnp.zeros((C,), jnp.float32), 'o_w': jax.random.normal(ks[4], (C, C), jnp.float32) * s, 'o_b': jnp.zeros((C,), jnp.float32), 'ln2_w': jnp.ones((C,), jnp.float32), 'ln2_b': jnp.zeros((C,), jnp.float32), 'fc_w': jax.random.normal(ks[5], (MW, C), jnp.float32) * s, 'fc_b': jnp.zeros((MW,), jnp.float32), 'proj_w': jax.random.normal(ks[6], (C, MW), jnp.float32) * s, 'proj_b': jnp.zeros((C,), jnp.float32)}
    _L0_attn_all = _L0_attn_setup()
    _L0_attn_in = {k: v for k, v in _L0_attn_all.items() if k in ('ln1_w', 'ln1_b', 'q_w', 'q_b', 'k_w', 'k_b', 'v_w', 'v_b', 'o_w', 'o_b', 'ln2_w', 'ln2_b', 'fc_w', 'fc_b', 'proj_w', 'proj_b')}
    del _L0_attn_all

    def _L0_ffn_setup():
        import jax, jax.numpy as jnp
        import numpy as np
        E = 16
        F_C = 2.0
        D = 256
        I = 4 * D
        IS = 2 * D
        B, S = (4, 256)
        key = jax.random.key(seed)
        ks = jax.random.split(key, 8)
        w = 0.02
        return {'hidden_states': jax.random.normal(ks[0], (B, S, D), dtype=jnp.float32), 'gate_w': jax.random.normal(ks[1], (E, D), dtype=jnp.float32) * w, 'Wg': jax.random.normal(ks[2], (E, I, D), dtype=jnp.float32) * w, 'Wu': jax.random.normal(ks[3], (E, I, D), dtype=jnp.float32) * w, 'Wd': jax.random.normal(ks[4], (E, D, I), dtype=jnp.float32) * w, 'Sg': jax.random.normal(ks[5], (IS, D), dtype=jnp.float32) * w, 'Su': jax.random.normal(ks[6], (IS, D), dtype=jnp.float32) * w, 'Sd': jax.random.normal(ks[7], (D, IS), dtype=jnp.float32) * w}
    _L0_ffn_all = _L0_ffn_setup()
    _L0_ffn_in = {k: v for k, v in _L0_ffn_all.items() if k in ('gate_w', 'Wg', 'Wu', 'Wd', 'Sg', 'Su', 'Sd')}
    del _L0_ffn_all
    return {'x': x, 'L0_tok_W': _L0_tok_in['W'], 'L0_tok_b': _L0_tok_in['b'], 'L0_tok_class_token': _L0_tok_in['class_token'], 'L0_tok_pos_embedding': _L0_tok_in['pos_embedding'], 'L0_attn_ln1_w': _L0_attn_in['ln1_w'], 'L0_attn_ln1_b': _L0_attn_in['ln1_b'], 'L0_attn_q_w': _L0_attn_in['q_w'], 'L0_attn_q_b': _L0_attn_in['q_b'], 'L0_attn_k_w': _L0_attn_in['k_w'], 'L0_attn_k_b': _L0_attn_in['k_b'], 'L0_attn_v_w': _L0_attn_in['v_w'], 'L0_attn_v_b': _L0_attn_in['v_b'], 'L0_attn_o_w': _L0_attn_in['o_w'], 'L0_attn_o_b': _L0_attn_in['o_b'], 'L0_attn_ln2_w': _L0_attn_in['ln2_w'], 'L0_attn_ln2_b': _L0_attn_in['ln2_b'], 'L0_attn_fc_w': _L0_attn_in['fc_w'], 'L0_attn_fc_b': _L0_attn_in['fc_b'], 'L0_attn_proj_w': _L0_attn_in['proj_w'], 'L0_attn_proj_b': _L0_attn_in['proj_b'], 'L0_ffn_gate_w': _L0_ffn_in['gate_w'], 'L0_ffn_Wg': _L0_ffn_in['Wg'], 'L0_ffn_Wu': _L0_ffn_in['Wu'], 'L0_ffn_Wd': _L0_ffn_in['Wd'], 'L0_ffn_Sg': _L0_ffn_in['Sg'], 'L0_ffn_Su': _L0_ffn_in['Su'], 'L0_ffn_Sd': _L0_ffn_in['Sd']}

def reference(x, L0_tok_W, L0_tok_b, L0_tok_class_token, L0_tok_pos_embedding, L0_attn_ln1_w, L0_attn_ln1_b, L0_attn_q_w, L0_attn_q_b, L0_attn_k_w, L0_attn_k_b, L0_attn_v_w, L0_attn_v_b, L0_attn_o_w, L0_attn_o_b, L0_attn_ln2_w, L0_attn_ln2_b, L0_attn_fc_w, L0_attn_fc_b, L0_attn_proj_w, L0_attn_proj_b, L0_ffn_gate_w, L0_ffn_Wg, L0_ffn_Wu, L0_ffn_Wd, L0_ffn_Sg, L0_ffn_Su, L0_ffn_Sd):
    import jax
    import jax.numpy as jnp

    def _L0_tok_ref(x, W, b, class_token, pos_embedding):
        import jax, jax.numpy as jnp
        import numpy as np
        P = 16

        def _patchify(x):
            B, C, H, W = x.shape
            gh, gw = (H // P, W // P)
            x = x.reshape(B, C, gh, P, gw, P)
            x = x.transpose(0, 2, 4, 1, 3, 5)
            return x.reshape(B, gh * gw, C * P * P)
        patches = _patchify(x)
        proj = jnp.einsum('bnk,dk->bnd', patches, W) + b
        B = x.shape[0]
        cls = jnp.broadcast_to(class_token, (B, 1, proj.shape[-1]))
        out = jnp.concatenate([cls, proj], axis=1) + pos_embedding
        return out

    def _L0_attn_ref(x, ln1_w, ln1_b, q_w, q_b, k_w, k_b, v_w, v_b, o_w, o_b, ln2_w, ln2_b, fc_w, fc_b, proj_w, proj_b):
        import jax, jax.numpy as jnp
        import numpy as np
        EPS = 1e-05

        def layer_norm(x, w, b):
            mu = jnp.mean(x, axis=-1, keepdims=True)
            var = jnp.var(x, axis=-1, keepdims=True)
            return (x - mu) / jnp.sqrt(var + EPS) * w + b
        B, N, C = x.shape
        H = 16
        D = C // H
        xn = layer_norm(x, ln1_w, ln1_b)
        q = (xn @ q_w.T + q_b).reshape(B, N, H, D).transpose(0, 2, 1, 3)
        k = (xn @ k_w.T + k_b).reshape(B, N, H, D).transpose(0, 2, 1, 3)
        v = (xn @ v_w.T + v_b).reshape(B, N, H, D).transpose(0, 2, 1, 3)
        q = jax.nn.elu(q) + 1.0
        k = jax.nn.elu(k) + 1.0
        kv = jnp.einsum('bhnd,bhne->bnde', k, v)
        qkv = jnp.einsum('bhnd,bnde->bhne', q, kv)
        k_sum = k.sum(axis=1)
        qk = jnp.einsum('bhnd,bnd->bhn', q, k_sum)
        attn = qkv / qk[..., None]
        attn = attn.transpose(0, 2, 1, 3).reshape(B, N, C)
        attn = attn @ o_w.T + o_b
        x = x + attn
        xn2 = layer_norm(x, ln2_w, ln2_b)
        h = jax.nn.gelu(xn2 @ fc_w.T + fc_b, approximate=False)
        x = x + (h @ proj_w.T + proj_b)
        return x

    def _L0_ffn_ref(hidden_states, gate_w, Wg, Wu, Wd, Sg, Su, Sd):
        import jax, jax.numpy as jnp
        import numpy as np
        E = 16
        F_C = 2.0
        D = 256
        I = 4 * D
        IS = 2 * D
        B, S = (4, 256)
        b, s, d = hidden_states.shape
        T = b * s
        C = int(T * F_C / E)
        flat_x = hidden_states.reshape(T, d)
        logits = flat_x @ gate_w.T
        scores = jax.nn.softmax(logits, axis=-1).T
        topk_weight, topk_idx = jax.lax.top_k(scores, C)
        xg = flat_x[topk_idx]
        g = jnp.einsum('ecd,eid->eci', xg, Wg)
        u = jnp.einsum('ecd,eid->eci', xg, Wu)
        h = jax.nn.gelu(g, approximate=False) * u
        eo = jnp.einsum('eci,edi->ecd', h, Wd)
        eo = eo * topk_weight[..., None]
        flat_out = jnp.zeros_like(flat_x).at[topk_idx.reshape(-1)].add(eo.reshape(-1, d))
        out = flat_out.reshape(b, s, d)
        sg = hidden_states @ Sg.T
        su = hidden_states @ Su.T
        shared = jax.nn.gelu(sg, approximate=False) * su @ Sd.T
        return out + shared
    h = _L0_tok_ref(x, L0_tok_W, L0_tok_b, L0_tok_class_token, L0_tok_pos_embedding)
    h = h + _L0_attn_ref(_layernorm(h, axis=-1), L0_attn_ln1_w, L0_attn_ln1_b, L0_attn_q_w, L0_attn_q_b, L0_attn_k_w, L0_attn_k_b, L0_attn_v_w, L0_attn_v_b, L0_attn_o_w, L0_attn_o_b, L0_attn_ln2_w, L0_attn_ln2_b, L0_attn_fc_w, L0_attn_fc_b, L0_attn_proj_w, L0_attn_proj_b)
    h = h + _L0_ffn_ref(_layernorm(h, axis=-1), L0_ffn_gate_w, L0_ffn_Wg, L0_ffn_Wu, L0_ffn_Wd, L0_ffn_Sg, L0_ffn_Su, L0_ffn_Sd)
    return h

_drawn_inputs = setup_inputs


def setup_inputs(seed=0):
    import zlib

    import numpy as np

    out = dict(_drawn_inputs(seed))
    spreads = {'L0_attn_ln1_w': (1.0, 0.6),
     'L0_attn_ln1_b': (0.0, 0.8),
     'L0_attn_q_b': (0.0, 0.8),
     'L0_attn_k_b': (0.0, 0.8),
     'L0_attn_v_b': (0.0, 0.8),
     'L0_attn_o_b': (0.0, 0.1),
     'L0_attn_ln2_w': (1.0, 0.6),
     'L0_attn_ln2_b': (0.0, 0.8),
     'L0_attn_fc_b': (0.0, 0.359),
     'L0_attn_proj_b': (0.0, 0.1)}
    factors = {'L0_attn_q_w': 8.0,
     'L0_attn_k_w': 8.0,
     'L0_attn_v_w': 3.221,
     'L0_attn_o_w': 3.05,
     'L0_ffn_gate_w': 8.0,
     'L0_ffn_Wg': 8.0,
     'L0_ffn_Wu': 8.0,
     'L0_ffn_Wd': 8.0,
     'L0_ffn_Sg': 3.602,
     'L0_ffn_Su': 3.496,
     'L0_ffn_Sd': 3.51}
    for name, (base, spread) in spreads.items():
        noise = np.random.default_rng([zlib.crc32(name.encode()), seed]).standard_normal(out[name].shape)
        drawn = base * np.exp(spread * noise) if base else spread * noise
        out[name] = jnp.asarray(drawn.astype(out[name].dtype))
    for name, factor in factors.items():
        out[name] = (out[name] * factor).astype(out[name].dtype)
    return out
```

```python
from contextlib import ExitStack

import numpy as np

import concourse.bass as bass
from concourse import mybir

P = 128
IMAGES, GRID, PATCH_K = 32, 36, 768
SEQ = GRID + 1
T = IMAGES * SEQ
TILES = -(-T // P)
TP = TILES * P
D = 256
KC = D // P
TKC = PATCH_K // P
H, HD = 16, 16
HE = HD + 1
MLP = 1024
MC = MLP // P
E = 16
C = int(T * 2.0 / E)
HC = C // 2
SH = 512
SC = SH // P
ROW = D + E
BASE = SEQ + 2
BITS = 30
NOWHERE = 4096.0
PAIRS = MC // 2
WGU = 2 * KC * MLP
WEX = WGU + MC * D
EPS = 1e-5

COL_LN1W, COL_LN1B, COL_LN2W, COL_LN2B, COL_FCB = 0, 2, 4, 6, 8
COLS = 16
K_ID, K_TRI = 0, P
K_CHUNK = 2 * P
K_PART = K_CHUNK + TILES * E
K_LIM = K_PART + TILES * E
K_IOTA = K_LIM + TILES * E
KCOLS = K_IOTA + HC

F32 = mybir.dt.float32
BF16 = mybir.dt.bfloat16
I32 = mybir.dt.int32
U32 = mybir.dt.uint32
ALU = mybir.AluOpType
ACT = mybir.ActivationFunctionType
AX = mybir.AxisListType.X


class Step:

    def __init__(self, i, c):
        self.i, self.c, self.par = i, c, c % 2

    @property
    def n(self):
        return self.i * 2 + self.c

    @property
    def half(self):
        return self.i + self.c // 2

    def off(self, k):
        return Step(self.i, self.c + k)

    def times(self, per, plus):
        return self.i * (2 * per) + (self.c * per + plus)


def vit_tower(nc, patches, sel, wtok, base, wqkv, bqkv, wo, bo, wfc, wproj, bproj, cols, gate,
              wsh, wsd, wex, consts, out):
    with ExitStack() as ctx:
        def sb(name, shape, dt=F32):
            return ctx.enter_context(nc.sbuf_tensor(name, shape, dt))

        def sem(name):
            return ctx.enter_context(nc.semaphore(name))

        bank = [ctx.enter_context(nc.psum_tensor(f"bank{n}", [P, 512], F32)) for n in range(8)]
        ps_tok, ps_tr, ps_qk, ps_v, ps_o = bank[0], bank[1], bank[2], bank[3], bank[4]
        ps_fc, ps_proj = (bank[5], bank[6]), bank[7]
        ps_logit, ps_count, ps_prefix, ps_slot = bank[0], bank[1], bank[0], bank[1]
        ps_gate, ps_up, ps_down = (bank[2], bank[5]), (bank[3], bank[6]), (bank[4], bank[7])
        ps_xt, ps_ot = bank[0], bank[1]

        rows = nc.dram_tensor("token_rows", (TP, ROW), F32).ap()

        kst = sb("kst", [P, KCOLS])
        ident = kst[:, K_ID:K_ID + P]
        colc = sb("colc", [P, COLS])
        ones_row = sb("ones_row", [1, P])
        nhalf = sb("nhalf", [P, 1])
        tri_b = sb("tri_b", [P, P], BF16)
        ones_b = sb("ones_b", [P, P], BF16)
        wtok_s = sb("wtok_s", [P, TKC, D])
        base_s = sb("base_s", [BASE, D])
        wqkv_s = sb("wqkv_s", [P, KC, 3 * D])
        bqkv_s = sb("bqkv_s", [1, 3 * D])
        wo_s = sb("wo_s", [P, KC, D])
        bo_s = sb("bo_s", [1, D])
        wfc_s = sb("wfc_s", [P, KC, MLP])
        wproj_s = sb("wproj_s", [P, MC, D])
        bproj_s = sb("bproj_s", [1, D])
        gate_s = sb("gate_s", [P, KC, E])
        wsh_s = sb("wsh_s", [P, KC, 2 * SH])
        wsd_s = sb("wsd_s", [P, SC, D])
        wex_s = [sb(f"wex_s{b}", [P, WEX]) for b in range(2)]

        patch_s = [sb(f"patch_s{b}", [P, TKC, P]) for b in range(2)]
        sel_s = [sb(f"sel_s{b}", [BASE, P]) for b in range(2)]
        h_all = sb("h_all", [P, TILES, D])
        x_all = sb("x_all", [P, TILES, D])
        hx = sb("hx", [P, D])
        stats = sb("stats", [P, 3, 6])
        mv = sb("mv", [P, 3, 2])
        tmp = sb("tmp", [P, 6])
        rstd = sb("rstd", [P, 4])
        xh = [sb(f"xh{b}", [P, D]) for b in range(2)]
        x2 = [sb(f"x2{b}", [P, D]) for b in range(2)]
        y_s = [sb(f"y_s{b}", [P, D]) for b in range(2)]
        xnT = sb("xnT", [P, KC, P])
        x2T = sb("x2T", [P, KC, P])
        attnT = sb("attnT", [P, KC, P])
        hidT = sb("hidT", [P, MC, P])
        neg = sb("neg", [P, 2 * D])
        expo = sb("expo", [P, 2 * D])
        qk = [sb(f"qk{b}", [P, 2 * D]) for b in range(2)]
        vx = [sb(f"vx{b}", [P, HE, H]) for b in range(2)]
        scratch = sb("scratch", [P, SC * TP])
        prod = scratch[:, 0:HD * HE * H]
        kv = sb("kv", [P, HE, HD])
        num = sb("num", [P, H, HE])
        rden = sb("rden", [P, H])
        attn = sb("attn", [P, D])
        yT = sb("yT", [P, KC, TP])

        mx = sb("mx", [P, TILES])
        score = sb("score", [P, TILES, E])
        sums = sb("sums", [P, TILES])
        cand = sb("cand", [P, E], I32)
        flip = sb("flip", [P, E], I32)
        cmp = sb("cmp", [P, TILES, E], BF16)
        ge = sb("ge", [P, TILES, 2, E], BF16)
        gef = sb("gef", [P, 2, TILES, E])
        pos = sb("pos", [P, TILES, E])
        pos2 = sb("pos2", [P, TILES, E])
        cgt = sb("cgt", [P, E])
        onehot = sb("onehot", [P, TILES, E // 4, HC], BF16)
        digits = sb("digits", [P, TILES, E, 4], BF16)
        slotf = sb("slotf", [HC, E, 4])
        slot = sb("slot", [HC, E, 2], U32)
        gel_sh = sb("gel_sh", [P, 512])
        hshT = scratch[:].rearrange("p (m t) -> p m t", m=SC)
        o_init = [sb(f"o_init{b}", [P, D]) for b in range(2)]

        slot_g = [sb(f"slot_g{b}_{k}", [HC, 1], U32) for b in range(2) for k in range(2)]
        slot_s = [sb(f"slot_s{b}_{k}", [HC, 1], U32) for b in range(2) for k in range(2)]
        weight = [sb(f"weight{b}_{k}", [HC, 1]) for b in range(2) for k in range(2)]
        xg = [sb(f"xg{b}_{k}", [HC, ROW]) for b in range(2) for k in range(2)]
        taken = 0

        def part(n):
            nonlocal taken
            taken += n
            assert taken <= SC * TP
            return scratch[:, taken - n:taken]

        xgT = [part(KC * C).rearrange("p (k c) -> p k c", k=KC) for _ in range(2)]
        gel = [part(2 * C) for _ in range(2)]
        hexT = part(MC * C).rearrange("p (m c) -> p m c", m=MC)
        eoT = part(KC * C).rearrange("p (k c) -> p k c", k=KC)
        eo = [part(D)[0:HC] for _ in range(4)]

        w_in = {n: sem(f"in_{n}") for n in ("consts", "tok", "qkv", "o", "fc", "proj", "moe")}
        patch_in = [sem(f"patch_in{b}") for b in range(2)]
        gu_in = [sem(f"gu_in{b}") for b in range(2)]
        dn_in = [sem(f"dn_in{b}") for b in range(2)]
        y_out = [sem(f"y_out{b}") for b in range(2)]
        score_out = sem("score_out")
        init_out = [sem(f"init_out{b}") for b in range(2)]
        ones_made, casts_made = sem("ones_made"), sem("casts_made")
        tok_done, h_copied = sem("tok_done"), sem("h_copied")
        a_stats, a_rstd, x0_made, xh_made = sem("a_stats"), sem("a_rstd"), sem("x0_made"), sem("xh_made")
        xh_turned, xnT_made = sem("xh_turned"), sem("xnT_made")
        qkv_done, neg_made, exp_made, v_made = sem("qkv_done"), sem("neg_made"), sem("exp_made"), sem("v_made")
        qk_made, attn_made = sem("qk_made"), sem("attn_made")
        attn_turned, attnT_made, o_done = sem("attn_turned"), sem("attnT_made"), sem("o_done")
        x1_made, c_stats, c_rstd, x2_made = sem("x1_made"), sem("c_stats"), sem("c_rstd"), sem("x2_made")
        x2_turned, x2T_made = sem("x2_turned"), sem("x2T_made")
        fc_done, hid_made = sem("fc_done"), sem("hid_made")
        proj_done, hx_made, h2_made = sem("proj_done"), sem("hx_made"), sem("h2_made")
        f_stats, f_rstd, y_made = sem("f_stats"), sem("f_rstd"), sem("y_made")
        y_turned, yT_made = sem("y_turned"), sem("yT_made")
        v_passed, p_passed = sem("v_passed"), sem("p_passed")
        v_chain, p_chain = sem("v_chain"), sem("p_chain")
        logits_done, centred, exps_made, scores_made = sem("logits_done"), sem("centred"), sem("exps_made"), sem("scores_made")
        cmp_made, counted = sem("cmp_made"), sem("counted")
        split_made, prefixed = sem("split_made"), sem("prefixed")
        digits_made, hot_made, slots_done, slots_made = sem("digits_made"), sem("hot_made"), sem("slots_done"), sem("slots_made")
        sgu_done, sgel_made, shid_made = sem("sgu_done"), sem("sgel_made"), sem("shid_made")
        sd_done, init_made = sem("sd_done"), sem("init_made")
        slot_copied = sem("slot_copied")
        row_in = [sem(f"row_in{b}") for b in range(2)]
        x_turned, xgT_made = sem("x_turned"), sem("xgT_made")
        egu_done, egel_made, ehid_made = sem("egu_done"), sem("egel_made"), sem("ehid_made")
        down_done, eoT_made, e_turned, eo_made = sem("down_done"), sem("eoT_made"), sem("e_turned"), sem("eo_made")
        scattered, weight_made = sem("scattered"), sem("weight_made")

        block = ctx.enter_context(nc.Block())

        SPAN = [(0, 512), (512, 512), (1024, 256)]
        SHARED = [(lo, n, m) for lo, n in SPAN for m in range(SC)]

        @block.sync
        def _(sp):
            def load_patch(s):
                sp.dma_start(patch_s[s.par][:], patches[s.n]).then_inc(patch_in[s.par], 16)
                sp.dma_start(sel_s[s.par][:], sel[s.n]).then_inc(patch_in[s.par], 16)

            load_patch(Step(0, 0))
            sp.dma_start(wtok_s[:], wtok).then_inc(w_in["tok"], 16)
            sp.dma_start(base_s[:], base).then_inc(w_in["tok"], 16)
            load_patch(Step(0, 1))
            sp.dma_start(wo_s[:], wo).then_inc(w_in["o"], 16)
            sp.dma_start(bo_s[:], bo).then_inc(w_in["o"], 16)
            sp.dma_start(wfc_s[:], wfc).then_inc(w_in["fc"], 16)
            sp.dma_start(wproj_s[:], wproj).then_inc(w_in["proj"], 16)
            sp.dma_start(bproj_s[:], bproj).then_inc(w_in["proj"], 16)

            def load_gu(s, e):
                sp.dma_start(wex_s[s.par][:, 0:WGU], wex[e, :, 0:WGU]).then_inc(gu_in[s.par], 16)

            def load_dn(s, e):
                sp.dma_start(wex_s[s.par][:, WGU:WEX], wex[e, :, WGU:WEX]).then_inc(dn_in[s.par], 16)

            def store_y(s):
                sp.wait_ge(y_made, s.times(1, 1))
                sp.dma_start(rows[bass.ds(s.n * P, P), 0:D], y_s[s.par][:]).then_inc(y_out[s.par], 16)

            def turn(s, first, last):
                if not last:
                    sp.wait_ge(tok_done, s.times(1, 1))
                    load_patch(s.off(2))
                if not first:
                    store_y(s.off(-1))

            turn(Step(0, 0), True, False)
            sp.dma_start(gate_s[:], gate).then_inc(w_in["moe"], 16)
            sp.dma_start(wsh_s[:], wsh).then_inc(w_in["moe"], 16)
            sp.dma_start(wsd_s[:], wsd).then_inc(w_in["moe"], 16)
            turn(Step(0, 1), False, False)
            for e in range(2):
                load_gu(Step(0, e), e)
                load_dn(Step(0, e), e)
            with sp.Fori(0, 3) as i:
                turn(Step(i, 2), False, False)
                turn(Step(i, 3), False, False)
            for c in range(TILES - 2, TILES + 1):
                turn(Step(0, c), False, True)
            sp.wait_ge(scores_made, 1)
            sp.dma_start(rows[:, D:ROW].rearrange("(t p) e -> p t e", p=P), score[:]).then_inc(score_out, 16)
            for t in range(TILES):
                sp.wait_ge(init_made, t + 1)
                sp.dma_start(out[t * P:(t + 1) * P, :], o_init[t % 2][:]).then_inc(init_out[t % 2], 16)
            with sp.Fori(0, E // 2 - 1) as i:
                for u in range(2):
                    s = Step(i, u)
                    sp.wait_ge(egu_done, s.times(PAIRS, PAIRS))
                    load_gu(s, s.n + 2)
                    sp.wait_ge(down_done, s.times(1, 1))
                    load_dn(s, s.n + 2)

        @block.gpsimd
        def _(gp):
            gp.memset(ones_row[:], 1.0)
            gp.memset(nhalf[:], -0.5)
            gp.memset(ones_b[:], 1.0)
            for b in range(2):
                last = gp.memset(vx[b][:], 1.0)
            last.then_inc(ones_made, 1)
            gp.wait_ge(ones_made, 1)

            def inverse_root(k, var, base_count):
                gp.sem_inc(p_passed, 1)
                gp.tensor_scalar(tmp[:, k:k + 1], var, EPS, None, ALU.add).then_inc(p_chain, 1)
                gp.wait_ge(p_chain, base_count(1))
                return gp.tensor_tensor(rstd[:, k:k + 1], tmp[:, k:k + 1], nhalf[:], ALU.pow)

            def norm_c(s, at):
                gp.wait_ge(c_stats, s.times(1, 1))
                inverse_root(1, mv[:, 1, 1:2], at).then_inc(c_rstd, 1)

            def norm_a(s, at):
                gp.wait_ge(a_stats, s.times(1, 1))
                inverse_root(0, mv[:, 0, 1:2], at).then_inc(p_chain, 1)
                gp.wait_ge(p_chain, at(2))
                gp.tensor_tensor(tmp[:, 4:5], rstd[:, 0:1], rstd[:, 0:1], ALU.mult).then_inc(p_chain, 1)
                gp.wait_ge(p_chain, at(3))
                gp.tensor_tensor(tmp[:, 5:6], tmp[:, 4:5], mv[:, 0, 1:2], ALU.mult).then_inc(p_chain, 1)
                gp.wait_ge(p_chain, at(4))
                inverse_root(3, tmp[:, 5:6], lambda k: at(4 + k)).then_inc(a_rstd, 1)

            def norm_f(s, at):
                gp.wait_ge(f_stats, s.times(1, 1))
                inverse_root(2, mv[:, 2, 1:2], at).then_inc(f_rstd, 1)

            def sum_hx(s):
                gp.wait_ge(x1_made, s.times(1, 1))
                gp.wait_ge(h2_made, s.times(1, 0))
                gp.tensor_tensor(hx[:], h_all[:, s.n, :], x_all[:, s.n, :], ALU.add).then_inc(hx_made, 1)

            norm_a(Step(0, 0), lambda k: k)

            def turn(s, first):
                at = lambda k: s.times(7, 3 + k)
                if not first:
                    norm_c(s.off(-1), at)
                    sum_hx(s.off(-1))
                norm_a(s.off(1), (lambda k: at(1 + k)) if not first else (lambda k: 5 + k))
                if not first:
                    norm_f(s.off(-1), lambda k: at(6 + k))

            turn(Step(0, 0), True)
            with gp.Fori(0, (TILES - 2) // 2) as i:
                turn(Step(i, 1), False)
                turn(Step(i, 2), False)
            count = 3 + 7 * (TILES - 1)
            for c in (TILES - 1, TILES):
                s = Step(0, c - 1)
                norm_c(s, lambda k: count + k)
                sum_hx(s)
                norm_f(s, lambda k: count + 1 + k)
                count += 2

            def gather(s, first):
                gp.wait_ge(slot_copied, s.times(2, 2))
                if not first:
                    gp.wait_ge(x_turned, s.times(1, -1))
                    gp.wait_ge(weight_made, s.times(2, -2))
                for k in range(2):
                    b = 2 * s.par + k
                    gp.sem_inc(p_passed, 1)
                    gp.indirect_dma_start(xg[b][:], None, rows, bass.IndirectOffsetOnAxis(slot_g[b][:], 0))\
                      .then_inc(row_in[s.par], 16)

            def scatter(s):
                gp.wait_ge(eo_made, s.times(2, 2))
                for k in range(2):
                    b = 2 * s.par + k
                    if k or not (isinstance(s.n, int) and s.n == 0):
                        gp.wait_ge(scattered, s.times(32, 16 * k))
                    gp.sem_inc(p_passed, 1)
                    gp.indirect_dma_start(out, bass.IndirectOffsetOnAxis(slot_s[b][:], 0), eo[b], None,
                                          compute_op=ALU.add).then_inc(scattered, 16)

            for b in range(2):
                gp.wait_ge(y_out[b], 16 * TILES // 2)
            gp.wait_ge(score_out, 16)
            gather(Step(0, 0), True)
            gather(Step(0, 1), True)
            for b in range(2):
                gp.wait_ge(init_out[b], 16 * TILES // 2)
            with gp.Fori(0, E // 2 - 1) as i:
                for u in (1, 2):
                    gather(Step(i, u + 1), False)
                    scatter(Step(i, u - 1))
            scatter(Step(0, E - 2))
            scatter(Step(0, E - 1))
            gp.wait_ge(scattered, 32 * E)

        @block.scalar
        def _(act):
            act.dma_start(kst[:], consts).then_inc(w_in["consts"], 16)
            act.dma_start(colc[:], cols).then_inc(w_in["consts"], 16)
            act.dma_start(wqkv_s[:], wqkv).then_inc(w_in["qkv"], 16)
            act.dma_start(bqkv_s[:], bqkv).then_inc(w_in["qkv"], 16)

            def copy_h(s):
                act.wait_ge(tok_done, s.times(1, 1))
                act.activation(h_all[:, s.n, :], ps_tok[:, 0:D], ACT.Copy).then_inc(h_copied, 1)

            def scale_xh(s):
                act.wait_ge(x0_made, s.times(1, 1))
                act.activation(xh[s.par][:], x_all[:, s.n, :], ACT.Copy, scale=rstd[:, 3:4]).then_inc(xh_made, 1)

            def affine(dst, w, b):
                for k in range(KC):
                    last = act.activation(dst[:, k, :], ps_tr[:, k * P:(k + 1) * P], ACT.Identity,
                                          scale=colc[:, w + k:w + k + 1], bias=colc[:, b + k:b + k + 1])
                return last

            def turn_xn(s):
                act.wait_ge(xh_turned, s.times(1, 1))
                affine(xnT, COL_LN1W, COL_LN1B).then_inc(xnT_made, 1)

            def qkv(s):
                act.wait_ge(qkv_done, s.times(1, 1))
                act.wait_ge(qk_made, s.times(1, 0))
                act.activation(neg[:], ps_qk[:], ACT.Relu, scale=-1.0).then_inc(neg_made, 1)
                act.activation(vx[s.par][:, 0:HD, :].rearrange("p e h -> p (e h)"), ps_v[:, 0:D],
                               ACT.Copy).then_inc(v_made, 1)
                act.wait_ge(neg_made, s.times(1, 1))
                act.activation(expo[:], neg[:], ACT.Exp, scale=-1.0).then_inc(exp_made, 1)

            def turn_attn(s):
                act.wait_ge(attn_turned, s.times(1, 1))
                act.activation(attnT[:].rearrange("p k t -> p (k t)"), ps_tr[:, 0:D], ACT.Copy).then_inc(attnT_made, 1)

            def turn_x2(s):
                act.wait_ge(x2_turned, s.times(1, 1))
                affine(x2T, COL_LN2W, COL_LN2B).then_inc(x2T_made, 1)

            def gelu(s):
                for g in range(2):
                    act.wait_ge(fc_done, s.times(2, g + 1))
                    for k in range(4):
                        m = 4 * g + k
                        last = act.activation(hidT[:, m, :], ps_fc[g][:, k * P:(k + 1) * P], ACT.Gelu,
                                              bias=colc[:, COL_FCB + m:COL_FCB + m + 1])
                    last.then_inc(hid_made, 1)

            def turn_y(s):
                act.wait_ge(y_turned, s.times(1, 1))
                act.activation(yT[:, :, bass.ds(s.n * P, P)], ps_tr[:, 0:D].rearrange("p (k t) -> p k t", k=KC),
                               ACT.Copy).then_inc(yT_made, 1)

            act.wait_ge(w_in["consts"], 32)
            copy_h(Step(0, 0))
            scale_xh(Step(0, 0))
            turn_xn(Step(0, 0))
            act.wait_ge(ones_made, 1)
            qkv(Step(0, 0))

            def turn(s, first, last):
                if not first:
                    turn_attn(s.off(-1))
                if not last:
                    copy_h(s.off(1))
                if not first:
                    turn_x2(s.off(-1))
                    gelu(s.off(-1))
                if not last:
                    scale_xh(s.off(1))
                    turn_xn(s.off(1))
                    qkv(s.off(1))
                if not first:
                    turn_y(s.off(-1))

            turn(Step(0, 0), True, False)
            with act.Fori(0, (TILES - 2) // 2) as i:
                turn(Step(i, 1), False, False)
                turn(Step(i, 2), False, False)
            turn(Step(0, TILES - 1), False, True)
            turn(Step(0, TILES), False, True)

            act.wait_ge(centred, 1)
            act.activation(score[:], score[:], ACT.Exp).then_inc(exps_made, 1)
            for j, (lo, n, m) in enumerate(SHARED):
                act.wait_ge(sgu_done, j + 1)
                if j:
                    act.wait_ge(shid_made, j)
                act.activation(gel_sh[:, 0:n], ps_gate[j % 2][:, 0:n], ACT.Gelu).then_inc(sgel_made, 1)

            def turn_x(s):
                act.wait_ge(x_turned, s.times(1, 1))
                act.activation(xgT[s.par].rearrange("p k c -> p (k c)"), ps_xt[:, 0:KC * C],
                               ACT.Copy).then_inc(xgT_made, 1)

            def gelu_e(s, p):
                act.wait_ge(egu_done, s.times(PAIRS, p + 1))
                act.activation(gel[p % 2], ps_gate[p % 2][:, 0:2 * C], ACT.Gelu).then_inc(egel_made, 1)

            def copy_eoT(s):
                act.wait_ge(down_done, s.times(1, 1))
                for k in range(KC):
                    last = act.activation(eoT[:, k, :], ps_down[k][:, 0:C], ACT.Copy)
                last.then_inc(eoT_made, 1)

            def expert(s, first, last):
                gelu_e(s, 0)
                if not first:
                    copy_eoT(s.off(-1))
                gelu_e(s, 1)
                gelu_e(s, 2)
                if not last:
                    turn_x(s.off(1))
                gelu_e(s, 3)

            turn_x(Step(0, 0))
            expert(Step(0, 0), True, False)
            with act.Fori(0, E // 2 - 1) as i:
                expert(Step(i, 1), False, False)
                expert(Step(i, 2), False, False)
            expert(Step(0, E - 1), False, True)
            copy_eoT(Step(0, E - 1))

        @block.vector
        def _(ve):
            ve.wait_ge(w_in["consts"], 32)
            ve.tensor_copy(tri_b[:], kst[:, K_TRI:K_TRI + P]).then_inc(casts_made, 1)

            def moments(k, src, at, done):
                ve.sem_inc(v_passed, 1)
                ve.bn_stats(stats[:, k, :], src).then_inc(v_chain, 1)
                ve.wait_ge(v_chain, at(1))
                ve.sem_inc(v_passed, 1)
                ve.bn_aggr(mv[:, k, :], stats[:, k, :]).then_inc(done, 1)

            def half_kv_product(s, g, at):
                if g == 0:
                    ve.wait_ge(v_made, s.times(1, 1))
                n = HD // 2
                k = qk[s.par][:, D:2 * D].rearrange("p (d h) -> p d h", h=H)[:, g * n:(g + 1) * n]
                ve.tensor_tensor(prod4[:, g * n:(g + 1) * n], k.unsqueeze(2).to_broadcast([P, n, HE, H]),
                                 vx[s.par][:].unsqueeze(1).to_broadcast([P, n, HE, H]), ALU.mult).then_inc(v_chain, 1)

            def half_kv_sum(s, g, at):
                n = HD // 2
                ve.wait_ge(v_chain, at)
                ve.tensor_reduce(kv[:].rearrange("p e d -> p d e")[:, g * n:(g + 1) * n], prod4[:, g * n:(g + 1) * n],
                                 AX, ALU.add).then_inc(v_chain, 1)

            def half_out_product(s, g, at):
                n = H // 2
                ve.wait_ge(v_chain, at)
                q = qk[s.par][:, 0:D].rearrange("p (h d) -> p h d", d=HD)[:, g * n:(g + 1) * n]
                ve.tensor_tensor(prodo[:, g * n:(g + 1) * n], q.unsqueeze(2).to_broadcast([P, n, HE, HD]),
                                 kv[:].unsqueeze(1).to_broadcast([P, n, HE, HD]), ALU.mult).then_inc(v_chain, 1)

            def half_out_sum(s, g, at):
                n = H // 2
                ve.wait_ge(v_chain, at)
                ve.tensor_reduce(num[:, g * n:(g + 1) * n, :], prodo[:, g * n:(g + 1) * n], AX, ALU.add).then_inc(v_chain, 1)

            prod4 = prod.rearrange("p (d e h) -> p d e h", d=HD, e=HE)
            prodo = prod.rearrange("p (h e d) -> p h e d", h=H, e=HE)

            def a_moments(s, at):
                ve.wait_ge(h_copied, s.times(1, 1))
                moments(0, h_all[:, s.n, :], at, a_stats)

            def a_scale(s):
                ve.wait_ge(a_rstd, s.times(1, 1))
                ve.wait_ge(a_stats, s.times(1, 1))
                ve.tensor_scalar(x_all[:, s.n, :], h_all[:, s.n, :], mv[:, 0, 0:1], rstd[:, 0:1],
                                 ALU.subtract, ALU.mult).then_inc(x0_made, 1)

            def c_moments(s, at):
                ve.wait_ge(o_done, s.times(1, 1))
                ve.tensor_tensor(x_all[:, s.n, :], ps_o[:, 0:D], x_all[:, s.n, :], ALU.add).then_inc(x1_made, 1)
                ve.wait_ge(x1_made, s.times(1, 1))
                moments(1, x_all[:, s.n, :], at, c_stats)

            def c_scale(s):
                ve.wait_ge(c_rstd, s.times(1, 1))
                ve.wait_ge(c_stats, s.times(1, 1))
                ve.tensor_scalar(x2[s.par][:], x_all[:, s.n, :], mv[:, 1, 0:1], rstd[:, 1:2],
                                 ALU.subtract, ALU.mult).then_inc(x2_made, 1)

            def f_moments(s, at):
                ve.wait_ge(proj_done, s.times(1, 1))
                ve.wait_ge(hx_made, s.times(1, 1))
                ve.tensor_tensor(h_all[:, s.n, :], ps_proj[:, 0:D], hx[:], ALU.add).then_inc(h2_made, 1)
                ve.wait_ge(h2_made, s.times(1, 1))
                moments(2, h_all[:, s.n, :], at, f_stats)

            def f_scale(s, has_older):
                ve.wait_ge(f_rstd, s.times(1, 1))
                ve.wait_ge(f_stats, s.times(1, 1))
                if has_older:
                    ve.wait_ge(y_out[s.par], s.half * 16)
                ve.tensor_scalar(y_s[s.par][:], h_all[:, s.n, :], mv[:, 2, 0:1], rstd[:, 2:3],
                                 ALU.subtract, ALU.mult).then_inc(y_made, 1)

            def combine(s):
                ve.wait_ge(exp_made, s.times(1, 1))
                ve.scalar_tensor_tensor(qk[s.par][:], ps_qk[:], 0.0, expo[:], ALU.max, ALU.add).then_inc(qk_made, 1)

            ve.wait_ge(ones_made, 1)
            a_moments(Step(0, 0), lambda k: k)
            a_scale(Step(0, 0))
            combine(Step(0, 0))
            CHAIN = 12

            def turn(s, first, last, attend=True):
                at0 = 1 if first else None
                at = (lambda k: 1 + k) if first else (lambda k: s.times(CHAIN, k - 1))
                n = 0
                if attend:
                    ve.wait_ge(qk_made, s.times(1, 1))
                    half_kv_product(s, 0, None)
                    n += 1
                    p0 = n
                if not first:
                    c_moments(s.off(-1), lambda k, n=n: at(n + k))
                    n += 1
                if attend:
                    half_kv_product(s, 1, None)
                    n += 1
                    p1 = n
                if not first:
                    c_scale(s.off(-1))
                if attend:
                    half_kv_sum(s, 0, at(p0))
                    n += 1
                if not last:
                    a_moments(s.off(1), lambda k, n=n: at(n + k))
                    n += 1
                if attend:
                    half_kv_sum(s, 1, at(p1))
                    n += 1
                    k1 = n
                if not last:
                    a_scale(s.off(1))
                if attend:
                    half_out_product(s, 0, at(k1))
                    n += 1
                    o0 = n
                    half_out_product(s, 1, at(k1))
                    n += 1
                    o1 = n
                if not first:
                    f_moments(s.off(-1), lambda k, n=n: at(n + k))
                    n += 1
                if attend:
                    half_out_sum(s, 0, at(o0))
                    n += 1
                if not first:
                    f_scale(s.off(-1), True if not isinstance(s.n, int) else s.n >= 3)
                if attend:
                    half_out_sum(s, 1, at(o1))
                    n += 1
                    ve.wait_ge(v_chain, at(n))
                    ve.reciprocal(rden[:], num[:, :, HD]).then_inc(v_chain, 1)
                    n += 1
                    ve.wait_ge(v_chain, at(n))
                    ve.tensor_tensor(attn[:].rearrange("p (h e) -> p h e", h=H), num[:, :, 0:HD],
                                     rden[:].unsqueeze(2).to_broadcast([P, H, HD]), ALU.mult).then_inc(attn_made, 1)
                if not last:
                    combine(s.off(1))
                return n

            n0 = turn(Step(0, 0), True, False)
            assert n0 == 10
            turn(Step(0, 1), False, False)
            turn(Step(0, 2), False, False)
            with ve.Fori(0, 3) as i:
                turn(Step(i, 3), False, False)
                turn(Step(i, 4), False, False)
            turn(Step(0, TILES - 1), False, True)
            chain = CHAIN * (TILES - 1) - 1 + 11
            s9 = Step(0, TILES - 1)
            c_moments(s9, lambda k: chain + k)
            c_scale(s9)
            f_moments(s9, lambda k: chain + 1 + k)
            f_scale(s9, True)
            chain += 2

            def link(ins):
                nonlocal chain
                chain += 1
                ins.then_inc(v_chain, 1)
                ve.wait_ge(v_chain, chain)

            lg = ps_logit[:, 0:TILES * E].rearrange("p (t e) -> p t e", e=E)
            ve.wait_ge(logits_done, 1)
            link(ve.tensor_reduce(mx[:], lg, AX, ALU.max))
            ve.tensor_tensor(score[:], lg, mx[:].unsqueeze(2).to_broadcast([P, TILES, E]), ALU.subtract).then_inc(centred, 1)
            ve.wait_ge(exps_made, 1)
            link(ve.tensor_reduce(sums[:], score[:], AX, ALU.add))
            link(ve.reciprocal(sums[:], sums[:]))
            link(ve.tensor_tensor(score[:], score[:], sums[:].unsqueeze(2).to_broadcast([P, TILES, E]), ALU.mult))
            lim = kst[:, K_LIM:K_LIM + TILES * E].rearrange("p (t e) -> p t e", e=E)
            ve.tensor_tensor(score[:], score[:], lim, ALU.min).then_inc(scores_made, 1)
            link(ve.memset(cand[:], 1 << (BITS - 1)))
            ve.wait_ge(scores_made, 1)

            def shared_hidden(j):
                lo, n, m = SHARED[j]
                ve.wait_ge(sgel_made, j + 1)
                ve.tensor_tensor(hshT[:, m, lo:lo + n], ps_up[j % 2][:, 0:n], gel_sh[:, 0:n], ALU.mult).then_inc(shid_made, 1)

            def shared_out(t):
                ve.wait_ge(sd_done, t + 1)
                if t >= 2:
                    ve.wait_ge(init_out[t % 2], 16 * (t // 2))
                ve.tensor_tensor(o_init[t % 2][:], ps_down[t % 2][:, 0:D], h_all[:, t, :], ALU.add).then_inc(init_made, 1)

            thr = cand[:].bitcast(F32)
            for r in range(BITS):
                bit = BITS - 1 - r
                ve.tensor_tensor(cmp[:], score[:], thr.unsqueeze(1).to_broadcast([P, TILES, E]), ALU.is_ge)\
                  .then_inc(cmp_made, 1)
                ve.wait_ge(counted, r + 1)
                link(ve.tensor_scalar(flip[:], ps_count[:, 0:E], C - 0.5, float(1 << bit), ALU.is_lt, ALU.mult))
                if bit:
                    link(ve.tensor_scalar(flip[:], flip[:], 1 << (bit - 1), None, ALU.bitwise_or))
                link(ve.tensor_tensor(cand[:], cand[:], flip[:], ALU.bitwise_xor))
                if r >= 2 and (r - 2) % 2 == 0 and (r - 2) // 2 < len(SHARED):
                    shared_hidden((r - 2) // 2)

            tb = thr.unsqueeze(1).to_broadcast([P, TILES, E])
            for k, op in enumerate((ALU.is_gt, ALU.is_equal)):
                ve.tensor_tensor(ge[:, :, k, :], score[:], tb, op).then_inc(split_made, 1)
                ve.tensor_tensor(gef[:, k, :, :], score[:], tb, op)
            ve.wait_ge(prefixed, 1)
            pf = ps_prefix[:, 0:TILES * 2 * E].rearrange("p (t k e) -> p t k e", k=2, e=E)
            link(ve.tensor_copy(cgt[:], ps_count[:, 0:E]))
            link(ve.tensor_tensor(pos[:], pf[:, :, 1, :], cgt[:].unsqueeze(1).to_broadcast([P, TILES, E]), ALU.add))
            flat = lambda ap: ap.rearrange("p t e -> p (t e)")
            link(ve.scalar_tensor_tensor(flat(pos[:]), flat(pos[:]), -NOWHERE, flat(gef[:, 1]), ALU.add, ALU.mult))
            link(ve.tensor_scalar(pos2[:], pf[:, :, 0, :], -NOWHERE, None, ALU.add))
            link(ve.tensor_tensor(pos2[:], pos2[:], gef[:, 0], ALU.mult))
            link(ve.scalar_tensor_tensor(flat(pos[:]), flat(pos[:]), NOWHERE, flat(pos2[:]), ALU.add, ALU.add))
            link(ve.tensor_scalar(gef[:, 1], pos[:], float(HC) - 0.5, None, ALU.is_gt))
            link(ve.tensor_scalar(gef[:, 0], pos[:], float(HC) - 0.5, None, ALU.is_lt))
            for k, col in enumerate((K_CHUNK, K_PART)):
                v = kst[:, col:col + TILES * E].rearrange("p (t e) -> p t e", e=E)
                for b in range(2):
                    last = ve.tensor_tensor(digits[:, :, :, 2 * k + b], gef[:, b], v, ALU.mult)
            last.then_inc(digits_made, 1)
            link(ve.scalar_tensor_tensor(flat(pos[:]), flat(gef[:, 1]), -float(HC), flat(pos[:]), ALU.mult, ALU.add))
            iota = kst[:, K_IOTA:K_IOTA + HC].unsqueeze(1).unsqueeze(1).to_broadcast([P, TILES, E // 4, HC])
            for q in range(4):
                if q:
                    ve.wait_ge(slots_done, q)
                a = pos[:, :, 4 * q:4 * q + 4].unsqueeze(3).to_broadcast([P, TILES, E // 4, HC])
                ve.tensor_tensor(onehot[:], a, iota, ALU.is_equal).then_inc(hot_made, 1)
                if q == 0:
                    shared_out(0)
                if q < 3:
                    shared_out(q + 1)
            ve.wait_ge(slots_done, 4)
            link(ve.tensor_copy(slotf[:].rearrange("p e k -> p (e k)"), ps_slot[0:HC, 0:4 * E]))
            link(ve.scalar_tensor_tensor(slot[:], slotf[:, :, 0:2], float(P), slotf[:, :, 2:4], ALU.mult, ALU.add))

            def copy_slot(s):
                for k in range(2):
                    ve.tensor_copy(slot_g[2 * s.par + k][:], slot[:, s.n, k:k + 1]).then_inc(slot_copied, 1)

            copy_slot(Step(0, 0))
            copy_slot(Step(0, 1))
            for t in range(4, TILES):
                shared_out(t)

            def hidden(s, p):
                ve.wait_ge(egel_made, s.times(PAIRS, p + 1))
                ve.tensor_tensor(hexT[:, 2 * p:2 * p + 2, :].rearrange("p m c -> p (m c)"),
                                 ps_up[p % 2][:, 0:2 * C], gel[p % 2], ALU.mult).then_inc(ehid_made, 1)

            def take_weight(s):
                if not (isinstance(s.n, int) and s.n < 2):
                    ve.wait_ge(eo_made, s.times(2, -2))
                ve.wait_ge(row_in[s.par], s.half * 32 + 32)
                for k in range(2):
                    ve.tensor_copy(weight[2 * s.par + k][:], xg[2 * s.par + k][:, bass.ds(s.n + D, 1)]).then_inc(weight_made, 1)

            def weigh(s):
                if not (isinstance(s.n, int) and s.n < 2):
                    ve.wait_ge(scattered, s.times(32, -32))
                for k in range(2):
                    ve.tensor_copy(slot_s[2 * s.par + k][:], slot[:, s.n, k:k + 1])
                ve.wait_ge(e_turned, s.times(1, 1))
                ve.wait_ge(weight_made, s.times(2, 2))
                for k in range(2):
                    ve.tensor_scalar(eo[2 * s.par + k], ps_ot[0:HC, k * D:(k + 1) * D],
                                     weight[2 * s.par + k][:], None, ALU.mult).then_inc(eo_made, 1)

            def expert(s, first, last):
                take_weight(s)
                hidden(s, 0)
                hidden(s, 1)
                if not first:
                    weigh(s.off(-1))
                hidden(s, 2)
                if not last:
                    copy_slot(s.off(2))
                hidden(s, 3)

            expert(Step(0, 0), True, False)
            expert(Step(0, 1), False, False)
            expert(Step(0, 2), False, False)
            with ve.Fori(0, E // 2 - 3) as i:
                expert(Step(i, 3), False, False)
                expert(Step(i, 4), False, False)
            expert(Step(0, E - 3), False, False)
            expert(Step(0, E - 2), False, True)
            expert(Step(0, E - 1), False, True)
            weigh(Step(0, E - 1))

        @block.tensor
        def _(pe):
            def turn_two(src, done):
                for k in range(KC):
                    last = pe.transpose(ps_tr[:, k * P:(k + 1) * P], src[:, k * P:(k + 1) * P], ident)
                last.then_inc(done, 1)

            def embed(s):
                pe.wait_ge(patch_in[s.par], s.half * 32 + 32)
                if not (isinstance(s.n, int) and s.n == 0):
                    pe.wait_ge(h_copied, s.times(1, 0))
                pe.matmul(ps_tok[:, 0:D], sel_s[s.par][:], base_s[:], start=True, stop=False)
                for k in range(TKC):
                    last = pe.matmul(ps_tok[:, 0:D], patch_s[s.par][:, k, :], wtok_s[:, k, :], start=False, stop=(k == TKC - 1))
                last.then_inc(tok_done, 1)

            def project_qkv(s):
                pe.wait_ge(xh_made, s.times(1, 1))
                turn_two(xh[s.par], xh_turned)
                pe.wait_ge(xnT_made, s.times(1, 1))
                if not (isinstance(s.n, int) and s.n == 0):
                    pe.wait_ge(qk_made, s.times(1, 0))
                    pe.wait_ge(v_made, s.times(1, 0))
                for dst, lo, n in ((ps_qk, 0, 2 * D), (ps_v, 2 * D, D)):
                    pe.matmul(dst[:, 0:n], ones_row[:], bqkv_s[:, lo:lo + n], start=True, stop=False)
                    for k in range(KC):
                        last = pe.matmul(dst[:, 0:n], xnT[:, k, :], wqkv_s[:, k, lo:lo + n], start=False, stop=(k == KC - 1))
                last.then_inc(qkv_done, 1)

            def project_attn(s):
                pe.wait_ge(attn_made, s.times(1, 1))
                if not (isinstance(s.n, int) and s.n == 0):
                    pe.wait_ge(yT_made, s.times(1, 0))
                turn_two(attn, attn_turned)
                pe.wait_ge(attnT_made, s.times(1, 1))
                if not (isinstance(s.n, int) and s.n == 0):
                    pe.wait_ge(x1_made, s.times(1, 0))
                pe.matmul(ps_o[:, 0:D], ones_row[:], bo_s[:], start=True, stop=False)
                for k in range(KC):
                    last = pe.matmul(ps_o[:, 0:D], attnT[:, k, :], wo_s[:, k, :], start=False, stop=(k == KC - 1))
                last.then_inc(o_done, 1)

            def mlp(s):
                pe.wait_ge(x2_made, s.times(1, 1))
                turn_two(x2[s.par], x2_turned)
                pe.wait_ge(x2T_made, s.times(1, 1))
                for m in range(MC):
                    for k in range(KC):
                        last = pe.matmul(ps_fc[m // 4][:, (m % 4) * P:(m % 4 + 1) * P], wfc_s[:, k, m * P:(m + 1) * P],
                                         x2T[:, k, :], start=(k == 0), stop=(k == KC - 1))
                    if m % 4 == 3:
                        last.then_inc(fc_done, 1)

            def project_mlp(s):
                if not (isinstance(s.n, int) and s.n == 0):
                    pe.wait_ge(h2_made, s.times(1, 0))
                pe.matmul(ps_proj[:, 0:D], ones_row[:], bproj_s[:], start=True, stop=False)
                for m in range(MC):
                    if m % 4 == 0:
                        pe.wait_ge(hid_made, s.times(2, m // 4 + 1))
                    last = pe.matmul(ps_proj[:, 0:D], hidT[:, m, :], wproj_s[:, m, :], start=False, stop=(m == MC - 1))
                last.then_inc(proj_done, 1)

            def turn_y(s):
                pe.wait_ge(y_made, s.times(1, 1))
                turn_two(y_s[s.par], y_turned)

            pe.wait_ge(w_in["tok"], 32)
            embed(Step(0, 0))
            pe.wait_ge(w_in["consts"], 32)
            pe.wait_ge(ones_made, 1)
            pe.wait_ge(w_in["qkv"], 32)
            project_qkv(Step(0, 0))

            def turn(s, first, last):
                if not first:
                    project_attn(s.off(-1))
                if not last:
                    embed(s.off(1))
                if not first:
                    mlp(s.off(-1))
                    project_mlp(s.off(-1))
                if not last:
                    project_qkv(s.off(1))
                if not first:
                    turn_y(s.off(-1))

            turn(Step(0, 0), True, False)
            pe.wait_ge(w_in["o"], 32)
            pe.wait_ge(w_in["fc"], 16)
            pe.wait_ge(w_in["proj"], 32)
            turn(Step(0, 1), False, False)
            turn(Step(0, 2), False, False)
            with pe.Fori(0, 3) as i:
                turn(Step(i, 3), False, False)
                turn(Step(i, 4), False, False)
            turn(Step(0, TILES - 1), False, True)
            turn(Step(0, TILES), False, True)

            pe.wait_ge(w_in["moe"], 48)
            pe.wait_ge(yT_made, TILES)
            pe.wait_ge(h_copied, TILES)
            for t in range(TILES):
                for k in range(KC):
                    last = pe.matmul(ps_logit[:, t * E:(t + 1) * E], yT[:, k, t * P:(t + 1) * P], gate_s[:, k, :],
                                     start=(k == 0), stop=(k == KC - 1))
            last.then_inc(logits_done, 1)

            def shared_gate_up(j):
                lo, n, m = SHARED[j]
                if j >= 2:
                    pe.wait_ge(shid_made, j - 1)
                for w, dst in ((0, ps_gate), (SH, ps_up)):
                    for k in range(KC):
                        last = pe.matmul(dst[j % 2][:, 0:n], wsh_s[:, k, w + m * P:w + (m + 1) * P], yT[:, k, lo:lo + n],
                                         start=(k == 0), stop=(k == KC - 1))
                        yield
                last.then_inc(sgu_done, 1)

            def shared_down(t):
                if t >= 2:
                    pe.wait_ge(init_made, t - 1)
                for m in range(SC):
                    last = pe.matmul(ps_down[t % 2][:, 0:D], hshT[:, m, t * P:(t + 1) * P], wsd_s[:, m, :],
                                     start=(m == 0), stop=(m == SC - 1))
                last.then_inc(sd_done, 1)

            pe.wait_ge(h2_made, TILES)
            for r in range(BITS):
                pe.wait_ge(cmp_made, r + 1)
                for t in range(TILES):
                    last = pe.matmul(ps_count[:, 0:E], ones_b[:], cmp[:, t, :], start=(t == 0), stop=(t == TILES - 1))
                last.then_inc(counted, 1)
                if r % 2 == 0 and r // 2 < len(SHARED):
                    for _ in shared_gate_up(r // 2):
                        pass
            pe.wait_ge(split_made, 2)
            pe.wait_ge(casts_made, 1)
            n = 2 * E
            g = ge[:].rearrange("p t k e -> p (t k e)")
            pe.matmul(ps_prefix[:, 0:TILES * n], tri_b[:], g, start=True, stop=False)
            for t in range(TILES - 1):
                left = TILES - 1 - t
                pe.matmul(ps_prefix[:, (t + 1) * n:TILES * n].rearrange("p (t c) -> p t c", c=n), ones_b[:],
                          g[:, t * n:(t + 1) * n].unsqueeze(1).to_broadcast([P, left, n]),
                          start=False, stop=(t == TILES - 2))
            for t in range(TILES):
                last = pe.matmul(ps_count[:, 0:E], ones_b[:], ge[:, t, 0, :], start=(t == 0), stop=(t == TILES - 1))
            last.then_inc(prefixed, 1)
            shared_down(0)
            shared_down(1)
            pe.wait_ge(digits_made, 1)
            for q in range(4):
                pe.wait_ge(hot_made, q + 1)
                for x in range(E // 4):
                    e = E // 4 * q + x
                    for t in range(TILES):
                        last = pe.matmul(ps_slot[0:HC, 4 * e:4 * e + 4], onehot[:, t, x, :], digits[:, t, e, :],
                                         start=(t == 0), stop=(t == TILES - 1))
                last.then_inc(slots_done, 1)
                if q < 3:
                    shared_down(2 + q)
            for t in range(5, TILES):
                shared_down(t)

            def turn_x(s):
                pe.wait_ge(row_in[s.par], s.half * 32 + 32)
                for b in range(2):
                    for k in range(KC):
                        last = pe.transpose(ps_xt[:, k * C + b * HC:k * C + (b + 1) * HC],
                                            xg[2 * s.par + b][:, k * P:(k + 1) * P], ident[0:HC, 0:HC])
                last.then_inc(x_turned, 1)

            def gate_up(s, p):
                if p == 0:
                    pe.wait_ge(gu_in[s.par], s.half * 16 + 16)
                    pe.wait_ge(xgT_made, s.times(1, 1))
                if not (isinstance(s.n, int) and s.n == 0 and p < 2):
                    pe.wait_ge(ehid_made, s.times(PAIRS, p - 1))
                for w, dst in ((0, ps_gate), (KC * MLP, ps_up)):
                    for x in range(2):
                        m = 2 * p + x
                        for k in range(KC):
                            lo = w + k * MLP + m * P
                            last = pe.matmul(dst[p % 2][:, x * C:(x + 1) * C], wex_s[s.par][:, lo:lo + P], xgT[s.par][:, k, :],
                                             start=(k == 0), stop=(k == KC - 1))
                last.then_inc(egu_done, 1)

            def down(s, p):
                if p == 0:
                    pe.wait_ge(dn_in[s.par], s.half * 16 + 16)
                pe.wait_ge(ehid_made, s.times(PAIRS, p + 1))
                for m in (2 * p, 2 * p + 1):
                    for k in range(KC):
                        lo = WGU + m * D + k * P
                        last = pe.matmul(ps_down[k][:, 0:C], wex_s[s.par][:, lo:lo + P], hexT[:, m, :],
                                         start=(m == 0), stop=(m == MC - 1))
                if p == PAIRS - 1:
                    last.then_inc(down_done, 1)

            def turn_eo(s):
                pe.wait_ge(eoT_made, s.times(1, 1))
                if not (isinstance(s.n, int) and s.n == 0):
                    pe.wait_ge(eo_made, s.times(2, 0))
                for b in range(2):
                    for k in range(KC):
                        last = pe.transpose(ps_ot[0:HC, b * D + k * P:b * D + (k + 1) * P], eoT[:, k, b * HC:(b + 1) * HC], ident)
                last.then_inc(e_turned, 1)

            def expert(s, first, last):
                gate_up(s, 0)
                if not first:
                    down(s.off(-1), PAIRS - 1)
                gate_up(s, 1)
                if not first:
                    turn_eo(s.off(-1))
                down(s, 0)
                gate_up(s, 2)
                if not last:
                    turn_x(s.off(1))
                down(s, 1)
                gate_up(s, 3)
                down(s, 2)

            turn_x(Step(0, 0))
            pe.wait_ge(init_made, TILES)
            pe.wait_ge(shid_made, len(SHARED))
            expert(Step(0, 0), True, False)
            with pe.Fori(0, E // 2 - 1) as i:
                expert(Step(i, 1), False, False)
                expert(Step(i, 2), False, False)
            expert(Step(0, E - 1), False, True)
            down(Step(0, E - 1), PAIRS - 1)
            turn_eo(Step(0, E - 1))


def _lay_out(inp):
    f = {k: np.asarray(v) for k, v in inp.items()}

    def chunks(w):
        return np.ascontiguousarray(w.T.reshape(-1, P, w.shape[0]).transpose(1, 0, 2))

    x = f["x"].reshape(IMAGES, 3, 6, 16, 6, 16).transpose(0, 2, 4, 1, 3, 5).reshape(IMAGES, GRID, PATCH_K)
    tok = np.zeros((TP, PATCH_K), x.dtype)
    tok[:T].reshape(IMAGES, SEQ, PATCH_K)[:, 1:] = x
    a = {"patches": np.ascontiguousarray(tok.reshape(TILES, P, TKC, P).transpose(0, 3, 2, 1))}

    sel = np.zeros((BASE, TP), np.float32)
    t = np.arange(T)
    sel[t % SEQ, t] = 1
    sel[np.where(t % SEQ == 0, SEQ + 1, SEQ), t] = 1
    a["sel"] = np.ascontiguousarray(sel.reshape(BASE, TILES, P).transpose(1, 0, 2))
    a["wtok"] = chunks(f["L0_tok_W"])
    a["base"] = np.concatenate([f["L0_tok_pos_embedding"][0], f["L0_tok_b"][None], f["L0_tok_class_token"][0]])
    turned = np.arange(D).reshape(H, HD).T.reshape(-1)
    order = [np.arange(D), turned, turned]
    ws = [f["L0_attn_%s_w" % n][o] for n, o in zip("qkv", order)]
    bs = [f["L0_attn_%s_b" % n][o] for n, o in zip("qkv", order)]
    a["wqkv"], a["bqkv"] = chunks(np.concatenate(ws)), np.concatenate(bs)[None]
    a["wo"], a["bo"] = chunks(f["L0_attn_o_w"]), f["L0_attn_o_b"][None]
    a["wfc"] = chunks(f["L0_attn_fc_w"])
    a["wproj"], a["bproj"] = chunks(f["L0_attn_proj_w"]), f["L0_attn_proj_b"][None]
    two = lambda v: v.reshape(-1, P).T
    a["cols"] = np.concatenate([two(f["L0_attn_" + n]) for n in ("ln1_w", "ln1_b", "ln2_w", "ln2_b", "fc_b")], axis=1)
    a["gate"] = chunks(f["L0_ffn_gate_w"])
    a["wsh"] = chunks(np.concatenate([f["L0_ffn_Sg"], f["L0_ffn_Su"]]))
    a["wsd"] = chunks(f["L0_ffn_Sd"])

    def expert_chunks(w):
        e, o, k = w.shape
        return w.transpose(0, 2, 1).reshape(e, k // P, P, o).transpose(0, 2, 1, 3).reshape(e, P, -1)

    a["wex"] = np.concatenate([expert_chunks(f["L0_ffn_" + n]) for n in ("Wg", "Wu", "Wd")], axis=2)
    c = np.zeros((P, KCOLS), np.float32)
    c[:, K_ID:K_ID + P] = np.eye(P)
    c[:, K_TRI:K_TRI + P] = np.triu(np.ones((P, P)), 1)
    tt = np.repeat(np.arange(TILES), E)
    c[:, K_CHUNK:K_CHUNK + TILES * E] = tt
    c[:, K_PART:K_PART + TILES * E] = np.arange(P)[:, None]
    c[:, K_LIM:K_LIM + TILES * E] = np.where(tt * P + np.arange(P)[:, None] < T, 2.0, -1.0)
    c[:, K_IOTA:] = np.arange(HC)
    a["consts"] = c
    return {k: np.ascontiguousarray(v) for k, v in a.items()}


_ORDER = ["patches", "sel", "wtok", "base", "wqkv", "bqkv", "wo", "bo", "wfc", "wproj", "bproj", "cols", "gate",
          "wsh", "wsd", "wex", "consts"]


def kernel(**inputs):
    import concourse.bacc as _bacc
    from concourse.bass_utils import run_bass_kernel_spmd as _run

    laid = _lay_out(inputs)
    nc = _bacc.Bacc("TRN2", target_bir_lowering=False, num_devices=1)
    args = [nc.dram_tensor(f"in_{n}", laid[n].shape, mybir.dt.from_np(laid[n].dtype), kind="ExternalInput").ap()
            for n in _ORDER]
    args.append(nc.dram_tensor("out_rows", (TP, D), F32, kind="ExternalOutput").ap())
    vit_tower(nc, *args)
    r = _run(nc, [{f"in_{n}": laid[n] for n in _ORDER}], core_ids=[0])
    return r.results[0]["out_rows"][:T].reshape(IMAGES, SEQ, D)
```

```python
from contextlib import ExitStack

import numpy as np

import concourse.bass as bass
from concourse import mybir

P = 128
IMAGES, GRID, PATCH_K = 32, 36, 768
SEQ = GRID + 1
T = IMAGES * SEQ
TILES = -(-T // P)
TP = TILES * P
D = 256
KC = D // P
TKC = PATCH_K // P
H, HD = 16, 16
HH = H // 2
MLP = 1024
MC = MLP // P
E = 16
C = int(T * 2.0 / E)
HC = C // 2
SH = 512
SC = SH // P
ROW = D + E
BASE = SEQ + 2
BITS = 30
NOWHERE = 4096.0
PAIRS = MC // 2
WGU = 2 * KC * MLP
WEX = WGU + MC * D
EPS = 1e-5

COL_LN1W, COL_LN1B, COL_LN2W, COL_LN2B, COL_FCB = 0, 2, 4, 6, 8
COLS = 16
B_QKV, B_O, B_PROJ, BIASES = 0, 3 * D, 4 * D, 5 * D
PARTS = (0, 32, 64)
BP = PARTS[-1] + 1
K_ID, K_TRI = 0, P
K_CHUNK = 2 * P
K_PART = K_CHUNK + TILES * E
K_LIM = K_PART + TILES * E
K_IOTA = K_LIM + TILES * E
KCOLS = K_IOTA + HC

F32 = mybir.dt.float32
BF16 = mybir.dt.bfloat16
I32 = mybir.dt.int32
U32 = mybir.dt.uint32
ALU = mybir.AluOpType
ACT = mybir.ActivationFunctionType
AX = mybir.AxisListType.X


class Step:

    def __init__(self, i, c):
        self.i, self.c, self.par = i, c, c % 2

    @property
    def n(self):
        return self.i * 2 + self.c

    @property
    def half(self):
        return self.i + self.c // 2

    def off(self, k):
        return Step(self.i, self.c + k)

    def times(self, per, plus):
        return self.i * (2 * per) + (self.c * per + plus)


def vit_tower(nc, patches, sel, wtok, base, wqkv, bias, wo, wfc, wproj, cols, gate,
              wsh, wsd, wex, consts, out):
    with ExitStack() as ctx:
        def sb(name, shape, dt=F32):
            return ctx.enter_context(nc.sbuf_tensor(name, shape, dt))

        def sem(name):
            return ctx.enter_context(nc.semaphore(name))

        bank = [ctx.enter_context(nc.psum_tensor(f"bank{n}", [P, 512], F32)) for n in range(8)]
        ps_tok, ps_tr, ps_qk, ps_v, ps_o = bank[0], bank[1], bank[2], bank[3], bank[4]
        ps_fc, ps_proj = (bank[5], bank[6]), bank[7]
        ps_num = bank[0][:, D:D + HH * HD]
        ps_xn, ps_y = bank[3][:, D:2 * D], bank[7][:, D:2 * D]
        ps_logit, ps_count, ps_prefix, ps_slot = bank[0], bank[1], bank[0], bank[1][:, E:5 * E]
        ps_shared = (bank[2], bank[3], bank[5], bank[6])
        ps_sd = [bank[b][:, h * D:(h + 1) * D] for b in (4, 7, 5, 6) for h in range(2)]
        ps_gate, ps_up, ps_down = (bank[2], bank[5]), (bank[3], bank[6]), (bank[4], bank[7])
        ps_xt, ps_ot = bank[0], bank[1]

        rows = nc.dram_tensor("token_rows", (TP, ROW), F32).ap()

        kst = sb("kst", [P, KCOLS])
        ident = kst[:, K_ID:K_ID + P]
        colc = sb("colc", [P, COLS])
        nhalf = sb("nhalf", [P, 1])
        minus = sb("minus", [P, 1])
        tri_b = sb("tri_b", [P, P], BF16)
        ones_b = sb("ones_b", [P, P], BF16)
        wtok_s = sb("wtok_s", [P, TKC, D])
        base_s = sb("base_s", [BASE, D])
        wqkv_s = sb("wqkv_s", [P, KC, 3 * D])
        bias_s = sb("bias_s", [BP, BIASES], BF16)
        wo_s = sb("wo_s", [P, KC, D])
        wfc_s = sb("wfc_s", [P, KC, MLP])
        wproj_s = sb("wproj_s", [P, MC, D])
        gate_s = sb("gate_s", [P, KC, E])
        wsh_s = sb("wsh_s", [P, KC, 2 * SH])
        wsd_s = sb("wsd_s", [P, SC, D])
        wex_s = [sb(f"wex_s{b}", [P, WEX]) for b in range(2)]

        patch_s = [sb(f"patch_s{b}", [P, TKC, P]) for b in range(2)]
        sel_s = [sb(f"sel_s{b}", [BASE, P]) for b in range(2)]
        h_all = sb("h_all", [P, TILES, D])
        x_all = sb("x_all", [P, TILES, D])
        hx = sb("hx", [P, D])
        stats = sb("stats", [P, 3, 6])
        mv = sb("mv", [P, 3, 2])
        tmp = sb("tmp", [P, 9])
        rstd = sb("rstd", [P, 4])
        shift = sb("shift", [P, 3])
        xh = [sb(f"xh{b}", [P, D]) for b in range(2)]
        x2 = [sb(f"x2{b}", [P, D]) for b in range(2)]
        y_s = [sb(f"y_s{b}", [P, D]) for b in range(2)]
        xnT = sb("xnT", [P, KC, P])
        x2T = sb("x2T", [P, KC, P])
        attnT = sb("attnT", [P, KC, P])
        hidT = sb("hidT", [P, MC, P])
        neg = sb("neg", [P, 2 * D])
        expo = sb("expo", [P, 2 * D])
        qk = [sb(f"qk{b}", [P, 2 * D]) for b in range(2)]
        vx = [sb(f"vx{b}", [P, HD, H]) for b in range(2)]
        scratch = sb("scratch", [P, SC * TP])
        prod = [scratch[:, g * HH * D:(g + 1) * HH * D] for g in range(2)]
        raw, rest = (scratch[0:BP, x * BIASES:(x + 1) * BIASES] for x in range(2))
        qkt = sb("qkt", [P, H, H])
        num = sb("num", [P, HH, HD])
        den = sb("den", [P, H])
        rden = sb("rden", [P, H])
        attn = sb("attn", [P, D])
        yT = sb("yT", [P, KC, TP])

        mx = sb("mx", [P, TILES])
        score = sb("score", [P, TILES, E])
        sums = sb("sums", [P, TILES])
        cand = sb("cand", [P, E], I32)
        flip = sb("flip", [P, E], I32)
        cmp = sb("cmp", [P, TILES, E], BF16)
        ge = sb("ge", [P, TILES, 2, E], BF16)
        gef = sb("gef", [P, 2, TILES, E])
        pos = sb("pos", [P, TILES, E])
        pos2 = sb("pos2", [P, TILES, E])
        cgt = sb("cgt", [P, E])
        onehot = [sb(f"onehot{b}", [P, TILES, 2, HC], BF16) for b in range(2)]
        digits = sb("digits", [P, TILES, E, 4], BF16)
        slotf = sb("slotf", [HC, E, 4])
        warm = sb("warm", [1, 2])
        slot = sb("slot", [HC, E, 2], U32)
        gel_sh = sb("gel_sh", [P, 512])
        hshT = scratch[:].rearrange("p (m t) -> p m t", m=SC)
        o_init = [sb(f"o_init{b}", [P, D]) for b in range(2)]

        slot_g = [sb(f"slot_g{b}_{k}", [HC, 1], U32) for b in range(2) for k in range(2)]
        slot_s = [sb(f"slot_s{b}_{k}", [HC, 1], U32) for b in range(2) for k in range(2)]
        weight = [sb(f"weight{b}_{k}", [HC, 1]) for b in range(2) for k in range(2)]
        xg = [sb(f"xg{b}_{k}", [HC, ROW]) for b in range(2) for k in range(2)]
        taken = 0

        def part(n):
            nonlocal taken
            taken += n
            assert taken <= SC * TP
            return scratch[:, taken - n:taken]

        xgT = [part(KC * C).rearrange("p (k c) -> p k c", k=KC) for _ in range(2)]
        gel = [part(2 * C) for _ in range(2)]
        hexT = part(MC * C).rearrange("p (m c) -> p m c", m=MC)
        eoT = part(KC * C).rearrange("p (k c) -> p k c", k=KC)
        eo = [part(D)[0:HC] for _ in range(4)]

        w_in = {n: sem(f"in_{n}") for n in ("bias", "consts", "tok", "qkv", "o", "fc", "proj", "moe")}
        patch_in = [sem(f"patch_in{b}") for b in range(2)]
        gu_in = [sem(f"gu_in{b}") for b in range(2)]
        dn_in = [sem(f"dn_in{b}") for b in range(2)]
        y_out = [sem(f"y_out{b}") for b in range(2)]
        score_out = sem("score_out")
        init_out = [sem(f"init_out{b}") for b in range(2)]
        ones_made, casts_made, bias_made = sem("ones_made"), sem("casts_made"), sem("bias_made")
        tok_done, h_copied = sem("tok_done"), sem("h_copied")
        a_stats, a_shift, a_rstd, x0_made, xh_made = sem("a_stats"), sem("a_shift"), sem("a_rstd"), sem("x0_made"), sem("xh_made")
        xh_turned, xnT_made = sem("xh_turned"), sem("xnT_made")
        qk_done, v_done, neg_made, exp_made, v_made = sem("qk_done"), sem("v_done"), sem("neg_made"), sem("exp_made"), sem("v_made")
        qk_made, attn_made = sem("qk_made"), sem("attn_made")
        prod_made, num_done = sem("prod_made"), sem("num_done")
        attn_turned, attnT_made, o_done = sem("attn_turned"), sem("attnT_made"), sem("o_done")
        x1_made, c_stats, c_rstd, x2_made = sem("x1_made"), sem("c_stats"), sem("c_rstd"), sem("x2_made")
        x2_turned, x2T_made = sem("x2_turned"), sem("x2T_made")
        fc_done, hid_made = sem("fc_done"), sem("hid_made")
        proj_done, hx_made, h2_made = sem("proj_done"), sem("hx_made"), sem("h2_made")
        f_stats, f_rstd, y_made = sem("f_stats"), sem("f_rstd"), sem("y_made")
        y_turned, yT_made = sem("y_turned"), sem("yT_made")
        v_passed, a_passed, p_passed = sem("v_passed"), sem("a_passed"), sem("p_passed")
        v_chain, p_chain = sem("v_chain"), sem("p_chain")
        logits_done, centred, exps_made, scores_made = sem("logits_done"), sem("centred"), sem("exps_made"), sem("scores_made")
        cmp_made, counted = sem("cmp_made"), sem("counted")
        split_made, prefixed = sem("split_made"), sem("prefixed")
        digits_made, hot_made, slots_done, slots_made = sem("digits_made"), sem("hot_made"), sem("slots_done"), sem("slots_made")
        sgu_done, sgel_made, shid_made = sem("sgu_done"), sem("sgel_made"), sem("shid_made")
        sd_done, init_made = sem("sd_done"), sem("init_made")
        slot_copied = sem("slot_copied")
        row_in = [sem(f"row_in{b}") for b in range(2)]
        x_turned, xgT_made = sem("x_turned"), sem("xgT_made")
        egu_done, egel_made, ehid_made = sem("egu_done"), sem("egel_made"), sem("ehid_made")
        down_done, eoT_made, e_turned, eo_made = sem("down_done"), sem("eoT_made"), sem("e_turned"), sem("eo_made")
        scattered, weight_made = sem("scattered"), sem("weight_made")

        block = ctx.enter_context(nc.Block())

        SPAN = 2 * P
        SHARED = [(lo, m) for lo in range(0, TP, SPAN) for m in range(SC)]
        EARLY = 3
        FILL = [4 * (len(SHARED) - EARLY) * r // BITS for r in range(BITS + 1)]
        HIDE = {r: [j for j in range(EARLY, len(SHARED))
                    if min(q for q in range(BITS) if FILL[q + 1] >= 4 * (j - EARLY + 1)) + 2 == r]
                for r in range(BITS + 2)}

        @block.sync
        def _(sp):
            def load_patch(s):
                sp.dma_start(patch_s[s.par][:], patches[s.n]).then_inc(patch_in[s.par], 16)
                sp.dma_start(sel_s[s.par][:], sel[s.n]).then_inc(patch_in[s.par], 16)

            load_patch(Step(0, 0))
            sp.dma_start(wtok_s[:], wtok).then_inc(w_in["tok"], 16)
            sp.dma_start(base_s[:], base).then_inc(w_in["tok"], 16)
            load_patch(Step(0, 1))
            sp.dma_start(wo_s[:], wo).then_inc(w_in["o"], 16)
            sp.dma_start(wfc_s[:], wfc).then_inc(w_in["fc"], 16)
            sp.dma_start(wproj_s[:], wproj).then_inc(w_in["proj"], 16)

            def load_gu(s, e):
                sp.dma_start(wex_s[s.par][:, 0:WGU], wex[e, :, 0:WGU]).then_inc(gu_in[s.par], 16)

            def load_dn(s, e):
                sp.dma_start(wex_s[s.par][:, WGU:WEX], wex[e, :, WGU:WEX]).then_inc(dn_in[s.par], 16)

            def store_y(s):
                sp.wait_ge(y_made, s.times(1, 1))
                sp.dma_start(rows[bass.ds(s.n * P, P), 0:D], y_s[s.par][:]).then_inc(y_out[s.par], 16)

            def next_patch(s):
                sp.wait_ge(tok_done, s.times(1, -1))
                load_patch(s)

            next_patch(Step(0, 2))
            sp.dma_start(gate_s[:], gate).then_inc(w_in["moe"], 16)
            sp.dma_start(wsh_s[:], wsh).then_inc(w_in["moe"], 16)
            sp.dma_start(wsd_s[:], wsd).then_inc(w_in["moe"], 16)
            next_patch(Step(0, 3))
            next_patch(Step(0, 4))
            for e in range(2):
                load_gu(Step(0, e), e)
                load_dn(Step(0, e), e)
            with sp.Fori(0, 2) as i:
                for c in (1, 2):
                    next_patch(Step(i, c + 4))
                    store_y(Step(i, c - 1))
            next_patch(Step(0, TILES - 1))
            for t in range(4, TILES):
                store_y(Step(0, t))
            sp.wait_ge(scores_made, 1)
            sp.dma_start(rows[:, D:ROW].rearrange("(t p) e -> p t e", p=P), score[:]).then_inc(score_out, 16)
            for t in range(TILES):
                sp.wait_ge(init_made, t + 1)
                sp.dma_start(out[t * P:(t + 1) * P, :], o_init[t % 2][:]).then_inc(init_out[t % 2], 16)
            with sp.Fori(0, E // 2 - 1) as i:
                for u in range(2):
                    s = Step(i, u)
                    sp.wait_ge(egu_done, s.times(PAIRS, PAIRS))
                    load_gu(s, s.n + 2)
                    sp.wait_ge(down_done, s.times(1, 1))
                    load_dn(s, s.n + 2)

        @block.gpsimd
        def _(gp):
            gp.memset(bias_s[:], 0.0)
            gp.memset(nhalf[:], -0.5)
            gp.memset(minus[:], -1.0)
            gp.memset(ones_b[:], 1.0)
            gp.memset(warm[:], 0.0).then_inc(ones_made, 1)
            gp.wait_ge(ones_made, 1)

            def inverse_root(k, var, base_count):
                gp.sem_inc(p_passed, 1)
                gp.tensor_scalar(tmp[:, k:k + 1], var, EPS, None, ALU.add).then_inc(p_chain, 1)
                gp.wait_ge(p_chain, base_count(1))
                return gp.tensor_tensor(rstd[:, k:k + 1], tmp[:, k:k + 1], nhalf[:], ALU.pow)

            def shift_of(k, at):
                gp.wait_ge(p_chain, at(2))
                gp.tensor_tensor(tmp[:, 6 + k:7 + k], rstd[:, k:k + 1], mv[:, k, 0:1], ALU.mult).then_inc(p_chain, 1)
                gp.wait_ge(p_chain, at(3))
                return gp.tensor_tensor(shift[:, k:k + 1], tmp[:, 6 + k:7 + k], minus[:], ALU.mult)

            def norm_c(s, at):
                gp.wait_ge(c_stats, s.times(1, 1))
                gp.wait_ge(x2_made, s.times(1, 0))
                inverse_root(1, mv[:, 1, 1:2], at).then_inc(p_chain, 1)
                shift_of(1, at).then_inc(c_rstd, 1)

            def norm_a(s, at):
                gp.wait_ge(a_stats, s.times(1, 1))
                gp.wait_ge(xh_made, s.times(1, 0))
                inverse_root(0, mv[:, 0, 1:2], at).then_inc(p_chain, 1)
                shift_of(0, at).then_inc(a_shift, 1)
                gp.tensor_tensor(tmp[:, 4:5], rstd[:, 0:1], rstd[:, 0:1], ALU.mult).then_inc(p_chain, 1)
                gp.wait_ge(p_chain, at(4))
                gp.tensor_tensor(tmp[:, 5:6], tmp[:, 4:5], mv[:, 0, 1:2], ALU.mult).then_inc(p_chain, 1)
                gp.wait_ge(p_chain, at(5))
                inverse_root(3, tmp[:, 5:6], lambda k: at(5 + k)).then_inc(a_rstd, 1)

            def norm_f(s, at):
                gp.wait_ge(f_stats, s.times(1, 1))
                gp.wait_ge(y_made, s.times(1, 0))
                inverse_root(2, mv[:, 2, 1:2], at).then_inc(p_chain, 1)
                shift_of(2, at).then_inc(f_rstd, 1)

            def sum_hx(s):
                gp.wait_ge(x1_made, s.times(1, 1))
                gp.wait_ge(h2_made, s.times(1, 0))
                gp.tensor_tensor(hx[:], h_all[:, s.n, :], x_all[:, s.n, :], ALU.add).then_inc(hx_made, 1)

            for t in range(3):
                norm_a(Step(0, t), lambda k, t=t: 6 * t + k)

            def turn(s):
                at = lambda k: s.times(12, 6 + k)
                norm_c(s.off(-1), at)
                sum_hx(s.off(-1))
                norm_a(s.off(2), lambda k: at(3 + k))
                norm_f(s.off(-1), lambda k: at(9 + k))

            with gp.Fori(0, 3) as i:
                turn(Step(i, 1))
                turn(Step(i, 2))
            turn(Step(0, 7))
            count = 6 + 12 * 8
            for c in (TILES - 2, TILES - 1, TILES):
                s = Step(0, c - 1)
                norm_c(s, lambda k: count + k)
                sum_hx(s)
                norm_f(s, lambda k: count + 3 + k)
                count += 6

            def gather(s, first):
                gp.wait_ge(slot_copied, s.times(2, 2))
                if not first:
                    gp.wait_ge(x_turned, s.times(1, -1))
                    gp.wait_ge(weight_made, s.times(2, -2))
                for k in range(2):
                    b = 2 * s.par + k
                    gp.sem_inc(p_passed, 1)
                    gp.indirect_dma_start(xg[b][:], None, rows, bass.IndirectOffsetOnAxis(slot_g[b][:], 0))\
                      .then_inc(row_in[s.par], 16)

            def scatter(s):
                gp.wait_ge(eo_made, s.times(2, 2))
                for k in range(2):
                    b = 2 * s.par + k
                    if k or not (isinstance(s.n, int) and s.n == 0):
                        gp.wait_ge(scattered, s.times(32, 16 * k))
                    gp.sem_inc(p_passed, 1)
                    gp.indirect_dma_start(out, bass.IndirectOffsetOnAxis(slot_s[b][:], 0), eo[b], None,
                                          compute_op=ALU.add).then_inc(scattered, 16)

            for b in range(2):
                gp.wait_ge(y_out[b], 16 * TILES // 2)
            gp.wait_ge(score_out, 16)
            gather(Step(0, 0), True)
            gather(Step(0, 1), True)
            for b in range(2):
                gp.wait_ge(init_out[b], 16 * TILES // 2)
            with gp.Fori(0, E // 2 - 1) as i:
                for u in (1, 2):
                    gather(Step(i, u + 1), False)
                    scatter(Step(i, u - 1))
            scatter(Step(0, E - 2))
            scatter(Step(0, E - 1))
            gp.wait_ge(scattered, 32 * E)

        @block.scalar
        def _(act):
            for q in PARTS:
                act.dma_start(raw[q:q + 1, :], bias).then_inc(w_in["bias"], 16)
            act.dma_start(kst[:], consts).then_inc(w_in["consts"], 16)
            act.dma_start(colc[:], cols).then_inc(w_in["consts"], 16)
            act.dma_start(wqkv_s[:], wqkv).then_inc(w_in["qkv"], 16)

            def copy_h(s):
                act.wait_ge(tok_done, s.times(1, 1))
                act.activation(h_all[:, s.n, :], ps_tok[:, 0:D], ACT.Copy).then_inc(h_copied, 1)

            def norm(dst, src, k, done):
                act.sem_inc(a_passed, 1)
                act.activation(dst, src, ACT.Identity, scale=rstd[:, k:k + 1], bias=shift[:, k:k + 1]).then_inc(done, 1)

            def norm_a(s):
                act.wait_ge(a_shift, s.times(1, 1))
                norm(x_all[:, s.n, :], h_all[:, s.n, :], 0, x0_made)

            def norm_c(s):
                act.wait_ge(c_rstd, s.times(1, 1))
                norm(x2[s.par][:], x_all[:, s.n, :], 1, x2_made)

            def norm_f(s, has_older=True):
                act.wait_ge(f_rstd, s.times(1, 1))
                if has_older:
                    act.wait_ge(y_out[s.par], s.half * 16)
                norm(y_s[s.par][:], h_all[:, s.n, :], 2, y_made)

            def scale_xh(s):
                act.wait_ge(a_rstd, s.times(1, 1))
                act.wait_ge(x0_made, s.times(1, 1))
                act.sem_inc(a_passed, 1)
                act.activation(xh[s.par][:], x_all[:, s.n, :], ACT.Copy, scale=rstd[:, 3:4]).then_inc(xh_made, 1)

            def affine(dst, src, w, b):
                for k in range(KC):
                    last = act.activation(dst[:, k, :], src[:, k * P:(k + 1) * P], ACT.Identity,
                                          scale=colc[:, w + k:w + k + 1], bias=colc[:, b + k:b + k + 1])
                return last

            def turn_xn(s):
                act.wait_ge(xh_turned, s.times(1, 1))
                affine(xnT, ps_xn, COL_LN1W, COL_LN1B).then_inc(xnT_made, 1)

            def negate_qk(s):
                act.wait_ge(qk_done, s.times(1, 1))
                act.wait_ge(qk_made, s.times(1, 0))
                act.activation(neg[:], ps_qk[:], ACT.Relu, scale=-1.0).then_inc(neg_made, 1)

            def exp_qk(s):
                act.wait_ge(neg_made, s.times(1, 1))
                act.activation(expo[:], neg[:], ACT.Exp, scale=-1.0).then_inc(exp_made, 1)

            def copy_v(s):
                act.wait_ge(v_done, s.times(1, 1))
                act.activation(vx[s.par][:].rearrange("p e h -> p (e h)"), ps_v[:, 0:D], ACT.Copy).then_inc(v_made, 1)

            def turn_attn(s):
                act.wait_ge(attn_turned, s.times(1, 1))
                act.activation(attnT[:].rearrange("p k t -> p (k t)"), ps_tr[:, 0:D], ACT.Copy).then_inc(attnT_made, 1)

            def turn_x2(s):
                act.wait_ge(x2_turned, s.times(1, 1))
                affine(x2T, ps_tr, COL_LN2W, COL_LN2B).then_inc(x2T_made, 1)

            def gelu(s):
                for g in range(2):
                    act.wait_ge(fc_done, s.times(2, g + 1))
                    for k in range(4):
                        m = 4 * g + k
                        last = act.activation(hidT[:, m, :], ps_fc[g][:, k * P:(k + 1) * P], ACT.Gelu,
                                              bias=colc[:, COL_FCB + m:COL_FCB + m + 1])
                    last.then_inc(hid_made, 1)

            def turn_y(s):
                act.wait_ge(y_turned, s.times(1, 1))
                act.activation(yT[:, :, bass.ds(s.n * P, P)], ps_y.rearrange("p (k t) -> p k t", k=KC),
                               ACT.Copy).then_inc(yT_made, 1)

            act.wait_ge(w_in["consts"], 32)
            copy_h(Step(0, 0))
            norm_a(Step(0, 0))
            scale_xh(Step(0, 0))
            copy_h(Step(0, 1))
            turn_xn(Step(0, 0))
            copy_v(Step(0, 0))
            negate_qk(Step(0, 0))
            exp_qk(Step(0, 0))
            norm_a(Step(0, 1))
            scale_xh(Step(0, 1))
            turn_xn(Step(0, 1))

            def load_exp():
                act.activation(warm[:, 1:2], warm[:, 0:1], ACT.Exp)

            def turn(s, older, prev, nxt, third):
                if nxt:
                    load_exp()
                if prev:
                    turn_attn(s.off(-1))
                if older:
                    norm_f(s.off(-2), not isinstance(s.n, int) or s.n >= 4)
                if nxt:
                    copy_v(s.off(1))
                    negate_qk(s.off(1))
                    exp_qk(s.off(1))
                if prev:
                    norm_c(s.off(-1))
                if older:
                    turn_y(s.off(-2))
                if prev:
                    turn_x2(s.off(-1))
                if third:
                    copy_h(s.off(2))
                if prev:
                    gelu(s.off(-1))
                if third:
                    norm_a(s.off(2))
                    scale_xh(s.off(2))
                    turn_xn(s.off(2))

            def gelu_shared(j):
                act.wait_ge(sgu_done, j + 1)
                if j >= 2:
                    act.wait_ge(shid_made, j - 1)
                act.activation(gel_sh[:, (j % 2) * SPAN:(j % 2 + 1) * SPAN], ps_shared[j % 4][:, 0:SPAN],
                               ACT.Gelu).then_inc(sgel_made, 1)

            turn(Step(0, 0), False, False, True, True)
            for c in (1, 2, 3):
                turn(Step(0, c), c > 1, True, True, True)
            with act.Fori(0, 2) as i:
                turn(Step(i, 4), True, True, True, True)
                turn(Step(i, 5), True, True, True, True)
            turn(Step(0, 8), True, True, True, False)
            turn(Step(0, 9), True, True, False, False)
            s9 = Step(0, TILES - 1)
            turn_attn(s9)
            norm_f(Step(0, TILES - 2))
            norm_c(s9)
            turn_y(Step(0, TILES - 2))
            gelu_shared(0)
            gelu_shared(1)
            turn_x2(s9)
            gelu(s9)
            norm_f(s9)
            gelu_shared(2)
            load_exp()
            turn_y(s9)

            act.wait_ge(centred, 1)
            act.activation(score[:], score[:], ACT.Exp).then_inc(exps_made, 1)
            for j in range(EARLY, len(SHARED)):
                gelu_shared(j)

            def turn_x(s):
                act.wait_ge(x_turned, s.times(1, 1))
                act.activation(xgT[s.par].rearrange("p k c -> p (k c)"), ps_xt[:, 0:KC * C],
                               ACT.Copy).then_inc(xgT_made, 1)

            def gelu_e(s, p):
                act.wait_ge(egu_done, s.times(PAIRS, p + 1))
                act.activation(gel[p % 2], ps_gate[p % 2][:, 0:2 * C], ACT.Gelu).then_inc(egel_made, 1)

            def copy_eoT(s):
                act.wait_ge(down_done, s.times(1, 1))
                for k in range(KC):
                    last = act.activation(eoT[:, k, :], ps_down[k][:, 0:C], ACT.Copy)
                last.then_inc(eoT_made, 1)

            def expert(s, first, last):
                gelu_e(s, 0)
                if not first:
                    copy_eoT(s.off(-1))
                gelu_e(s, 1)
                gelu_e(s, 2)
                if not last:
                    turn_x(s.off(1))
                gelu_e(s, 3)

            turn_x(Step(0, 0))
            expert(Step(0, 0), True, False)
            with act.Fori(0, E // 2 - 1) as i:
                expert(Step(i, 1), False, False)
                expert(Step(i, 2), False, False)
            expert(Step(0, E - 1), False, True)
            copy_eoT(Step(0, E - 1))

        @block.vector
        def _(ve):
            ve.wait_ge(w_in["bias"], 16 * len(PARTS))
            ve.wait_ge(ones_made, 1)
            step = 0
            for n, q in enumerate(PARTS):
                for k in range(n + 1):
                    src = raw if k == 0 else rest
                    ve.tensor_copy(bias_s[q:q + 1, :], src[q:q + 1, :]).then_inc(bias_made, 1)
                    step += 1
                    if k < n:
                        ve.wait_ge(bias_made, step)
                        ve.tensor_tensor(rest[q:q + 1, :], src[q:q + 1, :], bias_s[q:q + 1, :], ALU.subtract).then_inc(bias_made, 1)
                        step += 1
                        ve.wait_ge(bias_made, step)
            ve.wait_ge(w_in["consts"], 32)
            ve.tensor_copy(tri_b[:], kst[:, K_TRI:K_TRI + P]).then_inc(casts_made, 1)

            def moments(k, src, at, done):
                ve.sem_inc(v_passed, 1)
                ve.bn_stats(stats[:, k, :], src).then_inc(v_chain, 1)
                ve.wait_ge(v_chain, at(1))
                ve.sem_inc(v_passed, 1)
                ve.bn_aggr(mv[:, k, :], stats[:, k, :]).then_inc(done, 1)

            def heads(ap, g):
                return ap.rearrange("p (h d) -> p h d", d=HD)[:, g * HH:(g + 1) * HH]

            def qk_product(s, g):
                q = heads(qk[s.par][:, 0:D], g).unsqueeze(2).to_broadcast([P, HH, H, HD])
                k = qk[s.par][:, D:2 * D].rearrange("p (j d) -> p j d", d=HD).unsqueeze(1).to_broadcast([P, HH, H, HD])
                ve.tensor_tensor(prod[g].rearrange("p (h j d) -> p h j d", h=HH, j=H), q, k, ALU.mult).then_inc(v_chain, 1)

            def qk_sum(s, g, at):
                ve.wait_ge(v_chain, at)
                ve.tensor_reduce(qkt[:, g * HH:(g + 1) * HH, :], prod[g].rearrange("p (h j d) -> p h j d", h=HH, j=H),
                                 AX, ALU.add).then_inc(v_chain, 1)

            def v_product_pe(s, at):
                ve.wait_ge(v_made, s.times(1, 1))
                ve.wait_ge(v_chain, at)
                a = qkt[:, HH:, :].rearrange("p h j -> p j h").unsqueeze(3).to_broadcast([P, H, HH, HD])
                v = vx[s.par][:].rearrange("p e j -> p j e").unsqueeze(2).to_broadcast([P, H, HH, HD])
                ve.tensor_tensor(prod[1].rearrange("p (j h e) -> p j h e", j=H, h=HH), a, v, ALU.mult).then_inc(prod_made, 1)

            def v_product(s, at):
                ve.wait_ge(v_chain, at)
                a = qkt[:, 0:HH, :].unsqueeze(2).to_broadcast([P, HH, HD, H])
                v = vx[s.par][:].unsqueeze(1).to_broadcast([P, HH, HD, H])
                ve.tensor_tensor(prod[0].rearrange("p (h e j) -> p h e j", h=HH, e=HD), a, v, ALU.mult).then_inc(v_chain, 1)

            def v_sum(s, at):
                ve.wait_ge(v_chain, at)
                ve.tensor_reduce(num[:], prod[0].rearrange("p (h e j) -> p h e j", h=HH, e=HD), AX, ALU.add).then_inc(v_chain, 1)

            def divide(s, g, src):
                return ve.tensor_tensor(heads(attn[:], g), src, rden[:, g * HH:(g + 1) * HH].unsqueeze(2).to_broadcast([P, HH, HD]),
                                        ALU.mult)

            def a_moments(s, at):
                ve.wait_ge(h_copied, s.times(1, 1))
                ve.wait_ge(a_rstd, s.times(1, 0))
                moments(0, h_all[:, s.n, :], at, a_stats)

            def c_moments(s, at):
                ve.wait_ge(o_done, s.times(1, 1))
                ve.wait_ge(x0_made, s.times(1, 1))
                ve.tensor_tensor(x_all[:, s.n, :], ps_o[:, 0:D], x_all[:, s.n, :], ALU.add).then_inc(x1_made, 1)
                ve.wait_ge(x1_made, s.times(1, 1))
                ve.wait_ge(c_rstd, s.times(1, 0))
                moments(1, x_all[:, s.n, :], at, c_stats)

            def f_moments(s, at):
                ve.wait_ge(proj_done, s.times(1, 1))
                ve.wait_ge(hx_made, s.times(1, 1))
                ve.tensor_tensor(h_all[:, s.n, :], ps_proj[:, 0:D], hx[:], ALU.add).then_inc(h2_made, 1)
                ve.wait_ge(h2_made, s.times(1, 1))
                ve.wait_ge(f_rstd, s.times(1, 0))
                moments(2, h_all[:, s.n, :], at, f_stats)

            def combine(s):
                ve.wait_ge(exp_made, s.times(1, 1))
                ve.scalar_tensor_tensor(qk[s.par][:], ps_qk[:], 0.0, expo[:], ALU.max, ALU.add).then_inc(qk_made, 1)

            a_moments(Step(0, 0), lambda k: k)
            a_moments(Step(0, 1), lambda k: 1 + k)
            combine(Step(0, 0))
            CHAIN = 11

            def turn(s, at, prev, nxt, third):
                n = 0

                def gain():
                    nonlocal n
                    n += 1
                    return at(n)

                ve.wait_ge(qk_made, s.times(1, 1))
                qk_product(s, 1)
                product1 = gain()
                if prev:
                    c_moments(s.off(-1), lambda k, n=n: at(n + k))
                    gain()
                qk_product(s, 0)
                product0 = gain()
                qk_sum(s, 1, product1)
                sum1 = gain()
                if third:
                    a_moments(s.off(2), lambda k, n=n: at(n + k))
                    gain()
                qk_sum(s, 0, product0)
                sum0 = gain()
                v_product_pe(s, sum1)
                ve.wait_ge(v_chain, sum0)
                ve.tensor_reduce(den[:], qkt[:], AX, ALU.add).then_inc(v_chain, 1)
                summed = gain()
                if nxt:
                    combine(s.off(1))
                v_product(s, sum0)
                product0 = gain()
                ve.wait_ge(v_chain, summed)
                ve.reciprocal(rden[:], den[:]).then_inc(v_chain, 1)
                gain()
                v_sum(s, product0)
                done = gain()
                ve.wait_ge(v_chain, done)
                divide(s, 0, num[:])
                ve.wait_ge(num_done, s.times(1, 1))
                divide(s, 1, ps_num.rearrange("p (h e) -> p h e", e=HD)).then_inc(attn_made, 1)
                if prev:
                    f_moments(s.off(-1), lambda k, n=n: at(n + k))
                    gain()
                return n

            chain = 2
            chain += turn(Step(0, 0), lambda k: 2 + k, False, True, True)
            assert chain == CHAIN
            at = lambda s: lambda k: s.times(CHAIN, k)
            with ve.Fori(0, 3) as i:
                for c in (1, 2):
                    turn(Step(i, c), at(Step(i, c)), True, True, True)
            turn(Step(0, 7), at(Step(0, 7)), True, True, True)
            chain = CHAIN * 8
            chain += turn(Step(0, 8), lambda k: CHAIN * 8 + k, True, True, False)
            chain += turn(Step(0, 9), lambda k, c=chain: c + k, True, False, False)

            def shared_hidden(j):
                lo, m = SHARED[j]
                ve.wait_ge(sgel_made, j + 1)
                ve.tensor_tensor(hshT[:, m, lo:lo + SPAN], ps_shared[j % 4][:, SPAN:2 * SPAN],
                                 gel_sh[:, (j % 2) * SPAN:(j % 2 + 1) * SPAN], ALU.mult).then_inc(shid_made, 1)

            s9 = Step(0, TILES - 1)
            c_moments(s9, lambda k: chain + k)
            shared_hidden(0)
            shared_hidden(1)
            f_moments(s9, lambda k: chain + 1 + k)
            shared_hidden(2)
            chain += 2

            def link(ins):
                nonlocal chain
                chain += 1
                ins.then_inc(v_chain, 1)
                ve.wait_ge(v_chain, chain)

            lg = ps_logit[:, 0:TILES * E].rearrange("p (t e) -> p t e", e=E)
            ve.wait_ge(logits_done, 1)
            link(ve.tensor_reduce(mx[:], lg, AX, ALU.max))
            ve.tensor_tensor(score[:], lg, mx[:].unsqueeze(2).to_broadcast([P, TILES, E]), ALU.subtract).then_inc(centred, 1)
            ve.wait_ge(exps_made, 1)
            link(ve.tensor_reduce(sums[:], score[:], AX, ALU.add))
            link(ve.reciprocal(sums[:], sums[:]))
            link(ve.tensor_tensor(score[:], score[:], sums[:].unsqueeze(2).to_broadcast([P, TILES, E]), ALU.mult))
            lim = kst[:, K_LIM:K_LIM + TILES * E].rearrange("p (t e) -> p t e", e=E)
            ve.tensor_tensor(score[:], score[:], lim, ALU.min).then_inc(scores_made, 1)
            link(ve.memset(cand[:], 1 << (BITS - 1)))
            ve.wait_ge(scores_made, 1)

            def shared_out(t):
                ve.wait_ge(sd_done, (t | 1) + 1)
                if t >= 2:
                    ve.wait_ge(init_out[t % 2], 16 * (t // 2))
                ve.tensor_tensor(o_init[t % 2][:], ps_sd[t % 8], h_all[:, t, :], ALU.add).then_inc(init_made, 1)

            thr = cand[:].bitcast(F32)
            for r in range(BITS):
                bit = BITS - 1 - r
                ve.tensor_tensor(cmp[:], score[:], thr.unsqueeze(1).to_broadcast([P, TILES, E]), ALU.is_ge)\
                  .then_inc(cmp_made, 1)
                for j in HIDE[r]:
                    shared_hidden(j)
                ve.wait_ge(counted, r + 1)
                link(ve.tensor_scalar(flip[:], ps_count[:, 0:E], C - 0.5, float(1 << bit), ALU.is_lt, ALU.mult))
                if bit:
                    link(ve.scalar_tensor_tensor(cand[:], flip[:], 1 << (bit - 1), cand[:], ALU.bitwise_or, ALU.bitwise_xor))
                else:
                    link(ve.tensor_tensor(cand[:], cand[:], flip[:], ALU.bitwise_xor))

            tb = thr.unsqueeze(1).to_broadcast([P, TILES, E])
            for k, op in enumerate((ALU.is_gt, ALU.is_equal)):
                ve.tensor_tensor(ge[:, :, k, :], score[:], tb, op).then_inc(split_made, 1)
                ve.tensor_tensor(gef[:, k, :, :], score[:], tb, op)
            for j in HIDE[BITS] + HIDE[BITS + 1]:
                shared_hidden(j)
            ve.wait_ge(prefixed, 1)
            pf = ps_prefix[:, 0:TILES * 2 * E].rearrange("p (t k e) -> p t k e", k=2, e=E)
            link(ve.tensor_copy(cgt[:], ps_count[:, 0:E]))
            link(ve.tensor_tensor(pos[:], pf[:, :, 1, :], cgt[:].unsqueeze(1).to_broadcast([P, TILES, E]), ALU.add))
            flat = lambda ap: ap.rearrange("p t e -> p (t e)")
            link(ve.scalar_tensor_tensor(flat(pos[:]), flat(pos[:]), -NOWHERE, flat(gef[:, 1]), ALU.add, ALU.mult))
            link(ve.tensor_scalar(pos2[:], pf[:, :, 0, :], -NOWHERE, None, ALU.add))
            link(ve.tensor_tensor(pos2[:], pos2[:], gef[:, 0], ALU.mult))
            link(ve.scalar_tensor_tensor(flat(pos[:]), flat(pos[:]), NOWHERE, flat(pos2[:]), ALU.add, ALU.add))
            link(ve.tensor_scalar(gef[:, 1], pos[:], float(HC) - 0.5, None, ALU.is_gt))
            link(ve.tensor_scalar(gef[:, 0], pos[:], float(HC) - 0.5, None, ALU.is_lt))
            for k, col in enumerate((K_CHUNK, K_PART)):
                v = kst[:, col:col + TILES * E].rearrange("p (t e) -> p t e", e=E)
                for b in range(2):
                    last = ve.tensor_tensor(digits[:, :, :, 2 * k + b], gef[:, b], v, ALU.mult)
            last.then_inc(digits_made, 1)
            link(ve.scalar_tensor_tensor(flat(pos[:]), flat(gef[:, 1]), -float(HC), flat(pos[:]), ALU.mult, ALU.add))
            iota = kst[:, K_IOTA:K_IOTA + HC].unsqueeze(1).unsqueeze(1).to_broadcast([P, TILES, 2, HC])

            def hot(q):
                if q >= 2:
                    ve.wait_ge(slots_done, q - 1)
                a = pos[:, :, 2 * q:2 * q + 2].unsqueeze(3).to_broadcast([P, TILES, 2, HC])
                ve.tensor_tensor(onehot[q % 2][:], a, iota, ALU.is_equal).then_inc(hot_made, 1)

            def tokens(q):
                ve.wait_ge(slots_done, q + 1)
                f = slotf[:, 2 * q:2 * q + 2, :]
                ve.tensor_copy(f.rearrange("p e k -> p (e k)"), ps_slot[0:HC, 8 * q:8 * q + 8]).then_inc(slots_made, 1)
                ve.wait_ge(slots_made, q + 1)
                link(ve.scalar_tensor_tensor(slot[:, 2 * q:2 * q + 2, :], f[:, :, 0:2], float(P), f[:, :, 2:4], ALU.mult, ALU.add))

            def copy_slot(s):
                for k in range(2):
                    ve.tensor_copy(slot_g[2 * s.par + k][:], slot[:, s.n, k:k + 1]).then_inc(slot_copied, 1)

            hot(0)
            hot(1)
            tokens(0)
            copy_slot(Step(0, 0))
            copy_slot(Step(0, 1))
            for t in range(4):
                shared_out(t)
            tokens(1)
            for t in range(4, TILES):
                shared_out(t)

            def hidden(s, p):
                ve.wait_ge(egel_made, s.times(PAIRS, p + 1))
                ve.tensor_tensor(hexT[:, 2 * p:2 * p + 2, :].rearrange("p m c -> p (m c)"),
                                 ps_up[p % 2][:, 0:2 * C], gel[p % 2], ALU.mult).then_inc(ehid_made, 1)

            def take_weight(s):
                if not (isinstance(s.n, int) and s.n < 2):
                    ve.wait_ge(eo_made, s.times(2, -2))
                ve.wait_ge(row_in[s.par], s.half * 32 + 32)
                for k in range(2):
                    ve.tensor_copy(weight[2 * s.par + k][:], xg[2 * s.par + k][:, bass.ds(s.n + D, 1)]).then_inc(weight_made, 1)

            def weigh(s):
                if not (isinstance(s.n, int) and s.n < 2):
                    ve.wait_ge(scattered, s.times(32, -32))
                for k in range(2):
                    ve.tensor_copy(slot_s[2 * s.par + k][:], slot[:, s.n, k:k + 1])
                ve.wait_ge(e_turned, s.times(1, 1))
                ve.wait_ge(weight_made, s.times(2, 2))
                for k in range(2):
                    ve.tensor_scalar(eo[2 * s.par + k], ps_ot[0:HC, k * D:(k + 1) * D],
                                     weight[2 * s.par + k][:], None, ALU.mult).then_inc(eo_made, 1)

            def expert(s, first, last, hots=()):
                take_weight(s)
                hidden(s, 0)
                for q in hots[0:2]:
                    hot(q)
                hidden(s, 1)
                if not first:
                    weigh(s.off(-1))
                for q in hots[0:2]:
                    tokens(q)
                for q in hots[2:4]:
                    hot(q)
                hidden(s, 2)
                if not last:
                    copy_slot(s.off(2))
                for q in hots[2:4]:
                    tokens(q)
                for q in hots[4:6]:
                    hot(q)
                hidden(s, 3)
                for q in hots[4:6]:
                    tokens(q)

            expert(Step(0, 0), True, False, range(2, E // 2))
            expert(Step(0, 1), False, False)
            expert(Step(0, 2), False, False)
            with ve.Fori(0, E // 2 - 3) as i:
                expert(Step(i, 3), False, False)
                expert(Step(i, 4), False, False)
            expert(Step(0, E - 3), False, False)
            expert(Step(0, E - 2), False, True)
            expert(Step(0, E - 1), False, True)
            weigh(Step(0, E - 1))

        @block.tensor
        def _(pe):
            def turn_two(dst, src, done):
                for k in range(KC):
                    last = pe.transpose(dst[:, k * P:(k + 1) * P], src[:, k * P:(k + 1) * P], ident)
                last.then_inc(done, 1)

            def add_bias(dst, lo, n):
                pe.matmul(dst[:, 0:n], ones_b[0:BP, :], bias_s[:, lo:lo + n], start=True, stop=False)

            def embed(s, part=None):
                cut = TKC // 2
                if part != 1:
                    pe.wait_ge(patch_in[s.par], s.half * 32 + 32)
                    if not (isinstance(s.n, int) and s.n == 0):
                        pe.wait_ge(h_copied, s.times(1, 0))
                    pe.matmul(ps_tok[:, 0:D], sel_s[s.par][:], base_s[:], start=True, stop=False)
                for k in range(cut if part == 1 else 0, cut if part == 0 else TKC):
                    last = pe.matmul(ps_tok[:, 0:D], patch_s[s.par][:, k, :], wtok_s[:, k, :], start=False, stop=(k == TKC - 1))
                if part != 0:
                    last.then_inc(tok_done, 1)

            def turn_xh(s):
                pe.wait_ge(xh_made, s.times(1, 1))
                if not (isinstance(s.n, int) and s.n == 0):
                    pe.wait_ge(v_made, s.times(1, 0))
                turn_two(ps_xn, xh[s.par], xh_turned)

            def project_qk(s):
                if not (isinstance(s.n, int) and s.n == 0):
                    pe.wait_ge(qk_made, s.times(1, 0))
                add_bias(ps_qk, B_QKV, 2 * D)
                for k in range(KC):
                    last = pe.matmul(ps_qk[:], xnT[:, k, :], wqkv_s[:, k, 0:2 * D], start=False, stop=(k == KC - 1))
                last.then_inc(qk_done, 1)

            def project_v(s):
                pe.wait_ge(xnT_made, s.times(1, 1))
                add_bias(ps_v, B_QKV + 2 * D, D)
                for k in range(KC):
                    last = pe.matmul(ps_v[:, 0:D], xnT[:, k, :], wqkv_s[:, k, 2 * D:3 * D], start=False, stop=(k == KC - 1))
                last.then_inc(v_done, 1)

            def turn_attn(s):
                pe.wait_ge(attn_made, s.times(1, 1))
                turn_two(ps_tr, attn, attn_turned)

            def project_attn(s):
                pe.wait_ge(attnT_made, s.times(1, 1))
                if not (isinstance(s.n, int) and s.n == 0):
                    pe.wait_ge(x1_made, s.times(1, 0))
                add_bias(ps_o, B_O, D)
                for k in range(KC):
                    last = pe.matmul(ps_o[:, 0:D], attnT[:, k, :], wo_s[:, k, :], start=False, stop=(k == KC - 1))
                last.then_inc(o_done, 1)

            def turn_x2(s):
                pe.wait_ge(x2_made, s.times(1, 1))
                turn_two(ps_tr, x2[s.par], x2_turned)

            def mlp(s):
                pe.wait_ge(x2T_made, s.times(1, 1))
                for m in range(MC):
                    for k in range(KC):
                        last = pe.matmul(ps_fc[m // 4][:, (m % 4) * P:(m % 4 + 1) * P], wfc_s[:, k, m * P:(m + 1) * P],
                                         x2T[:, k, :], start=(k == 0), stop=(k == KC - 1))
                    if m % 4 == 3:
                        last.then_inc(fc_done, 1)

            def project_mlp(s):
                if not (isinstance(s.n, int) and s.n == 0):
                    pe.wait_ge(h2_made, s.times(1, 0))
                    pe.wait_ge(yT_made, s.times(1, 0))
                add_bias(ps_proj, B_PROJ, D)
                for m in range(MC):
                    if m % 4 == 0:
                        pe.wait_ge(hid_made, s.times(2, m // 4 + 1))
                    last = pe.matmul(ps_proj[:, 0:D], hidT[:, m, :], wproj_s[:, m, :], start=False, stop=(m == MC - 1))
                last.then_inc(proj_done, 1)

            def turn_y(s):
                pe.wait_ge(y_made, s.times(1, 1))
                turn_two(ps_y, y_s[s.par], y_turned)

            def sum_values(s):
                pe.wait_ge(prod_made, s.times(1, 1))
                pe.wait_ge(h_copied, TILES if isinstance(s.n, int) and s.n > TILES - 3 else s.times(1, 3))
                n = HH * HD
                for j in range(H):
                    last = pe.matmul(ps_num, ident, prod[1][:, j * n:(j + 1) * n], start=(j == 0), stop=(j == H - 1))
                last.then_inc(num_done, 1)

            pe.wait_ge(w_in["tok"], 32)
            embed(Step(0, 0))
            embed(Step(0, 1))
            pe.wait_ge(w_in["consts"], 32)
            turn_xh(Step(0, 0))
            pe.wait_ge(bias_made, 9)
            pe.wait_ge(w_in["qkv"], 16)
            project_v(Step(0, 0))
            project_qk(Step(0, 0))
            turn_xh(Step(0, 1))

            def turn(s, older, prev, nxt, third):
                if prev:
                    turn_attn(s.off(-1))
                if nxt:
                    project_v(s.off(1))
                if prev:
                    project_attn(s.off(-1))
                if nxt:
                    project_qk(s.off(1))
                if third:
                    embed(s.off(2), 0)
                if older:
                    turn_y(s.off(-2))
                if prev:
                    turn_x2(s.off(-1))
                if third:
                    embed(s.off(2), 1)
                if prev:
                    mlp(s.off(-1))
                    project_mlp(s.off(-1))
                if third:
                    turn_xh(s.off(2))
                sum_values(s)

            turn(Step(0, 0), False, False, True, True)
            pe.wait_ge(w_in["o"], 16)
            pe.wait_ge(w_in["fc"], 16)
            pe.wait_ge(w_in["proj"], 16)
            turn(Step(0, 1), False, True, True, True)
            with pe.Fori(0, 3) as i:
                turn(Step(i, 2), True, True, True, True)
                turn(Step(i, 3), True, True, True, True)
            turn(Step(0, 8), True, True, True, False)
            turn(Step(0, 9), True, True, False, False)

            def shared_gate_up(j):
                lo, m = SHARED[j]
                if j >= 4:
                    pe.wait_ge(shid_made, j - 3)
                for x in range(2):
                    for k in range(KC):
                        last = pe.matmul(ps_shared[j % 4][:, x * SPAN:(x + 1) * SPAN],
                                         wsh_s[:, k, x * SH + m * P:x * SH + (m + 1) * P], yT[:, k, lo:lo + SPAN],
                                         start=(k == 0), stop=(k == KC - 1))
                        if x == 1 and k == KC - 1:
                            last.then_inc(sgu_done, 1)
                        yield

            def logits(t):
                for k in range(KC):
                    last = pe.matmul(ps_logit[:, t * E:(t + 1) * E], yT[:, k, t * P:(t + 1) * P], gate_s[:, k, :],
                                     start=(k == 0), stop=(k == KC - 1))
                return last

            s9 = Step(0, TILES - 1)
            turn_attn(s9)
            project_attn(s9)
            turn_y(Step(0, TILES - 2))
            pe.wait_ge(w_in["moe"], 48)
            for j in range(2):
                for _ in shared_gate_up(j):
                    pass
            turn_x2(s9)
            mlp(s9)
            project_mlp(s9)
            for _ in shared_gate_up(2):
                pass
            for t in range(TILES - 1):
                logits(t)
            turn_y(s9)
            pe.wait_ge(yT_made, TILES)
            logits(TILES - 1).then_inc(logits_done, 1)

            def shared_down(t):
                if t >= 8:
                    pe.wait_ge(init_made, 2)
                for m in range(SC):
                    last = pe.matmul(ps_sd[t % 8], hshT[:, m, t * P:(t + 1) * P], wsd_s[:, m, :],
                                     start=(m == 0), stop=(m == SC - 1))
                last.then_inc(sd_done, 1)

            filler = (step for j in range(EARLY, len(SHARED)) for step in shared_gate_up(j))
            for r in range(BITS):
                pe.wait_ge(cmp_made, r + 1)
                for t in range(TILES):
                    last = pe.matmul(ps_count[:, 0:E], ones_b[:], cmp[:, t, :], start=(t == 0), stop=(t == TILES - 1))
                last.then_inc(counted, 1)
                for _ in range(FILL[r + 1] - FILL[r]):
                    next(filler)
            pe.wait_ge(split_made, 2)
            pe.wait_ge(casts_made, 1)
            n = 2 * E
            g = ge[:].rearrange("p t k e -> p (t k e)")
            pe.matmul(ps_prefix[:, 0:TILES * n], tri_b[:], g, start=True, stop=False)
            for t in range(TILES - 1):
                left = TILES - 1 - t
                pe.matmul(ps_prefix[:, (t + 1) * n:TILES * n].rearrange("p (t c) -> p t c", c=n), ones_b[:],
                          g[:, t * n:(t + 1) * n].unsqueeze(1).to_broadcast([P, left, n]),
                          start=False, stop=(t == TILES - 2))
            for t in range(TILES):
                last = pe.matmul(ps_count[:, 0:E], ones_b[:], ge[:, t, 0, :], start=(t == 0), stop=(t == TILES - 1))
            last.then_inc(prefixed, 1)

            def slots(q):
                pe.wait_ge(hot_made, q + 1)
                if q:
                    pe.wait_ge(slots_made, q)
                for e in (2 * q, 2 * q + 1):
                    for t in range(TILES):
                        last = pe.matmul(ps_slot[0:HC, 4 * e:4 * e + 4], onehot[q % 2][:, t, e % 2, :], digits[:, t, e, :],
                                         start=(t == 0), stop=(t == TILES - 1))
                last.then_inc(slots_done, 1)

            pe.wait_ge(shid_made, len(SHARED))
            for t in range(4):
                shared_down(t)
            pe.wait_ge(digits_made, 1)
            slots(0)
            shared_down(4)
            slots(1)
            for t in range(5, TILES):
                shared_down(t)

            def turn_x(s):
                pe.wait_ge(row_in[s.par], s.half * 32 + 32)
                for b in range(2):
                    for k in range(KC):
                        last = pe.transpose(ps_xt[:, k * C + b * HC:k * C + (b + 1) * HC],
                                            xg[2 * s.par + b][:, k * P:(k + 1) * P], ident[0:HC, 0:HC])
                last.then_inc(x_turned, 1)

            def gate_up(s, p):
                if p == 0:
                    pe.wait_ge(gu_in[s.par], s.half * 16 + 16)
                    pe.wait_ge(xgT_made, s.times(1, 1))
                if not (isinstance(s.n, int) and s.n == 0 and p < 2):
                    pe.wait_ge(ehid_made, s.times(PAIRS, p - 1))
                for w, dst in ((0, ps_gate), (KC * MLP, ps_up)):
                    for x in range(2):
                        m = 2 * p + x
                        for k in range(KC):
                            lo = w + k * MLP + m * P
                            last = pe.matmul(dst[p % 2][:, x * C:(x + 1) * C], wex_s[s.par][:, lo:lo + P], xgT[s.par][:, k, :],
                                             start=(k == 0), stop=(k == KC - 1))
                last.then_inc(egu_done, 1)

            def down(s, p):
                if p == 0:
                    pe.wait_ge(dn_in[s.par], s.half * 16 + 16)
                pe.wait_ge(ehid_made, s.times(PAIRS, p + 1))
                for m in (2 * p, 2 * p + 1):
                    for k in range(KC):
                        lo = WGU + m * D + k * P
                        last = pe.matmul(ps_down[k][:, 0:C], wex_s[s.par][:, lo:lo + P], hexT[:, m, :],
                                         start=(m == 0), stop=(m == MC - 1))
                if p == PAIRS - 1:
                    last.then_inc(down_done, 1)

            def turn_eo(s):
                pe.wait_ge(eoT_made, s.times(1, 1))
                if not (isinstance(s.n, int) and s.n == 0):
                    pe.wait_ge(eo_made, s.times(2, 0))
                pe.wait_ge(slots_made, E // 2)
                for b in range(2):
                    for k in range(KC):
                        last = pe.transpose(ps_ot[0:HC, b * D + k * P:b * D + (k + 1) * P], eoT[:, k, b * HC:(b + 1) * HC], ident)
                last.then_inc(e_turned, 1)

            def expert(s, first, last, hots=()):
                gate_up(s, 0)
                if not first:
                    down(s.off(-1), PAIRS - 1)
                gate_up(s, 1)
                if not first:
                    turn_eo(s.off(-1))
                for q in hots[0:2]:
                    slots(q)
                down(s, 0)
                gate_up(s, 2)
                if not last:
                    turn_x(s.off(1))
                for q in hots[2:4]:
                    slots(q)
                down(s, 1)
                gate_up(s, 3)
                for q in hots[4:6]:
                    slots(q)
                down(s, 2)

            turn_x(Step(0, 0))
            pe.wait_ge(init_made, TILES)
            expert(Step(0, 0), True, False, range(2, E // 2))
            with pe.Fori(0, E // 2 - 1) as i:
                expert(Step(i, 1), False, False)
                expert(Step(i, 2), False, False)
            expert(Step(0, E - 1), False, True)
            down(Step(0, E - 1), PAIRS - 1)
            turn_eo(Step(0, E - 1))


def _lay_out(inp):
    f = {k: np.asarray(v) for k, v in inp.items()}

    def chunks(w):
        return np.ascontiguousarray(w.T.reshape(-1, P, w.shape[0]).transpose(1, 0, 2))

    x = f["x"].reshape(IMAGES, 3, 6, 16, 6, 16).transpose(0, 2, 4, 1, 3, 5).reshape(IMAGES, GRID, PATCH_K)
    tok = np.zeros((TP, PATCH_K), x.dtype)
    tok[:T].reshape(IMAGES, SEQ, PATCH_K)[:, 1:] = x
    a = {"patches": np.ascontiguousarray(tok.reshape(TILES, P, TKC, P).transpose(0, 3, 2, 1))}

    sel = np.zeros((BASE, TP), np.float32)
    t = np.arange(T)
    sel[t % SEQ, t] = 1
    sel[np.where(t % SEQ == 0, SEQ + 1, SEQ), t] = 1
    a["sel"] = np.ascontiguousarray(sel.reshape(BASE, TILES, P).transpose(1, 0, 2))
    a["wtok"] = chunks(f["L0_tok_W"])
    a["base"] = np.concatenate([f["L0_tok_pos_embedding"][0], f["L0_tok_b"][None], f["L0_tok_class_token"][0]])
    turned = np.arange(D).reshape(H, HD).T.reshape(-1)
    order = [np.arange(D), np.arange(D), turned]
    ws = [f["L0_attn_%s_w" % n][o] for n, o in zip("qkv", order)]
    bs = [f["L0_attn_%s_b" % n][o] for n, o in zip("qkv", order)]
    a["wqkv"] = chunks(np.concatenate(ws))
    a["bias"] = np.concatenate(bs + [f["L0_attn_o_b"], f["L0_attn_proj_b"]])[None]
    a["wo"] = chunks(f["L0_attn_o_w"])
    a["wfc"] = chunks(f["L0_attn_fc_w"])
    a["wproj"] = chunks(f["L0_attn_proj_w"])
    two = lambda v: v.reshape(-1, P).T
    a["cols"] = np.concatenate([two(f["L0_attn_" + n]) for n in ("ln1_w", "ln1_b", "ln2_w", "ln2_b", "fc_b")], axis=1)
    a["gate"] = chunks(f["L0_ffn_gate_w"])
    a["wsh"] = chunks(np.concatenate([f["L0_ffn_Sg"], f["L0_ffn_Su"]]))
    a["wsd"] = chunks(f["L0_ffn_Sd"])

    def expert_chunks(w):
        e, o, k = w.shape
        return w.transpose(0, 2, 1).reshape(e, k // P, P, o).transpose(0, 2, 1, 3).reshape(e, P, -1)

    a["wex"] = np.concatenate([expert_chunks(f["L0_ffn_" + n]) for n in ("Wg", "Wu", "Wd")], axis=2)
    c = np.zeros((P, KCOLS), np.float32)
    c[:, K_ID:K_ID + P] = np.eye(P)
    c[:, K_TRI:K_TRI + P] = np.triu(np.ones((P, P)), 1)
    tt = np.repeat(np.arange(TILES), E)
    c[:, K_CHUNK:K_CHUNK + TILES * E] = tt
    c[:, K_PART:K_PART + TILES * E] = np.arange(P)[:, None]
    c[:, K_LIM:K_LIM + TILES * E] = np.where(tt * P + np.arange(P)[:, None] < T, 2.0, -1.0)
    c[:, K_IOTA:] = np.arange(HC)
    a["consts"] = c
    return {k: np.ascontiguousarray(v) for k, v in a.items()}


_ORDER = ["patches", "sel", "wtok", "base", "wqkv", "bias", "wo", "wfc", "wproj", "cols", "gate",
          "wsh", "wsd", "wex", "consts"]


def kernel(**inputs):
    import concourse.bacc as _bacc
    from concourse.bass_utils import run_bass_kernel_spmd as _run

    laid = _lay_out(inputs)
    nc = _bacc.Bacc("TRN2", target_bir_lowering=False, num_devices=1)
    args = [nc.dram_tensor(f"in_{n}", laid[n].shape, mybir.dt.from_np(laid[n].dtype), kind="ExternalInput").ap()
            for n in _ORDER]
    args.append(nc.dram_tensor("out_rows", (TP, D), F32, kind="ExternalOutput").ap())
    vit_tower(nc, *args)
    r = _run(nc, [{f"in_{n}": laid[n] for n in _ORDER}], core_ids=[0])
    return r.results[0]["out_rows"][:T].reshape(IMAGES, SEQ, D)
```

```python
from contextlib import ExitStack

import numpy as np

import concourse.bass as bass
from concourse import mybir

P = 128
IMAGES, GRID, PATCH_K = 32, 36, 768
SEQ = GRID + 1
T = IMAGES * SEQ
TILES = -(-T // P)
TP = TILES * P
D = 256
KC = D // P
TKC = PATCH_K // P
H, HD = 16, 16
HV = 7
HH = H // 2
MLP = 1024
MC = MLP // P
E = 16
C = int(T * 2.0 / E)
HC = C // 2
SH = 512
SC = SH // P
ROW = D + E
BASE = SEQ + 2
BITS = 30
ROUNDS = BITS // 2
NOWHERE = 4096.0
PAIRS = MC // 2
WGU = 2 * KC * MLP
WEX = WGU + MC * D
SCRATCH = max(H * D, (2 * KC + 4 + MC + KC + 2 * KC) * C + 4 * D)
EPS = 1e-5
WARM = 14

SPLIT = 256.0
HALVES = 8
COL_LN1W, COL_LN1B, COL_LN2W, COL_LN2B, COL_FCB = 0, 2, 4, 6, 8
COLS = 16
B_QKV, B_O, B_PROJ, BIASES = 0, 3 * D, 4 * D, 5 * D
PARTS = (0, 32, 64)
BP = PARTS[-1] + 1
K_ID, K_TRI = 0, P
K_CHUNK = 2 * P
K_PART = K_CHUNK + TILES * E
K_LIM = K_PART + TILES * E
K_IOTA = K_LIM + TILES * E
KCOLS = K_IOTA + HC

F32 = mybir.dt.float32
BF16 = mybir.dt.bfloat16
F16 = mybir.dt.float16
I32 = mybir.dt.int32
U32 = mybir.dt.uint32
ALU = mybir.AluOpType
ACT = mybir.ActivationFunctionType
AX = mybir.AxisListType.X


class Step:

    def __init__(self, i, c):
        self.i, self.c, self.par = i, c, c % 2

    @property
    def n(self):
        return self.i * 2 + self.c

    @property
    def half(self):
        return self.i + self.c // 2

    def off(self, k):
        return Step(self.i, self.c + k)

    def times(self, per, plus):
        return self.i * (2 * per) + (self.c * per + plus)


def vit_tower(nc, patches, sel, wtok, base, wqkv, bias, wo, wfc, wproj, cols, gate,
              wsh, wsd, wex, consts, out):
    with ExitStack() as ctx:
        def sb(name, shape, dt=F32):
            return ctx.enter_context(nc.sbuf_tensor(name, shape, dt))

        def sem(name):
            return ctx.enter_context(nc.semaphore(name))

        bank = [ctx.enter_context(nc.psum_tensor(f"bank{n}", [P, 512], F32)) for n in range(8)]
        ps_tok, ps_tr, ps_qk, ps_v, ps_o = bank[0], bank[1], bank[2], bank[3], bank[4]
        ps_fc, ps_proj = (bank[5], bank[6]), bank[7]
        ps_num = bank[0][:, D:D + (H - HV) * HD]
        ps_xn, ps_y = bank[3][:, D:2 * D], bank[7][:, D:2 * D]
        ps_logit, ps_count, ps_prefix, ps_slot = bank[0], bank[1], bank[0], bank[0][:, 320:320 + 4 * E]

        def ps_shared(j):
            return bank[(3, 2)[j % 2]] if j < EARLY else bank[(3, 2, 5, 6)[j % 4]]

        ps_sd = [bank[b][:, h * D:(h + 1) * D] for b in (4, 7, 5, 6) for h in range(2)]
        ps_gate, ps_up, ps_down = (bank[2], bank[5]), (bank[3], bank[6]), (bank[4], bank[7])
        ps_xt, ps_ot = bank[0], bank[1]

        rows = nc.dram_tensor("token_rows", (TP, ROW), F32).ap()

        parts = nc.dram_tensor("bias_parts", (len(PARTS), BIASES), BF16).ap()

        kst = sb("kst", [P, KCOLS])
        ident = kst[:, K_ID:K_ID + P]
        colc = sb("colc", [P, COLS])
        nhalf = sb("nhalf", [P, 1])
        minus = sb("minus", [P, 1])
        tri_b = sb("tri_b", [P, P], BF16)
        ones_b = sb("ones_b", [P, P], BF16)
        wtok_s = sb("wtok_s", [P, TKC, D])
        base_s = sb("base_s", [BASE, D])
        wqkv_s = sb("wqkv_s", [P, KC, 3 * D])
        braw, brest = sb("braw", [P, BIASES // P]), sb("brest", [P, BIASES // P])
        bpart = sb("bpart", [P, len(PARTS), BIASES // P], BF16)
        bias_s = sb("bias_s", [BP, BIASES], BF16)
        wo_s = sb("wo_s", [P, KC, D])
        wfc_s = sb("wfc_s", [P, KC, MLP])
        wproj_s = sb("wproj_s", [P, MC, D])
        gate_s = sb("gate_s", [P, KC, E])
        wsh_s = sb("wsh_s", [P, KC, 2 * SH])
        wsd_s = sb("wsd_s", [P, SC, D])
        wex_s = [sb(f"wex_s{b}", [P, WEX]) for b in range(2)]

        patch_s = [sb(f"patch_s{b}", [P, TKC, P]) for b in range(2)]
        sel_s = [sb(f"sel_s{b}", [BASE, P]) for b in range(2)]
        h_all = sb("h_all", [P, TILES, D])
        x_all = sb("x_all", [P, TILES, D])
        hx = sb("hx", [P, D])
        stats = sb("stats", [P, 3, 6])
        mv = sb("mv", [P, 3, 2])
        tmp = sb("tmp", [P, 9])
        rstd = sb("rstd", [P, 4])
        shift = sb("shift", [P, 3])
        xh = [sb(f"xh{b}", [P, D]) for b in range(2)]
        x2 = [sb(f"x2{b}", [P, D]) for b in range(2)]
        y_s = [sb(f"y_s{b}", [P, D]) for b in range(2)]
        xnT = sb("xnT", [P, KC, P])
        x2T = sb("x2T", [P, KC, P])
        attnT = sb("attnT", [P, KC, P])
        hidT = sb("hidT", [P, MC, P])
        neg = sb("neg", [P, 2 * D])
        expo = sb("expo", [P, 2 * D])
        qk = [sb(f"qk{b}", [P, 2 * D]) for b in range(2)]
        vx = [sb(f"vx{b}", [P, HD, H]) for b in range(2)]
        hsh_s = sb("hsh_s", [P, TP])
        scratch = sb("scratch", [P, SCRATCH])
        prod = [scratch[:, g * HH * D:(g + 1) * HH * D] for g in range(2)]
        prod_v = [scratch[:, 0:HV * D], scratch[:, HV * D:H * D]]
        qkt = sb("qkt", [P, H, H])
        num = sb("num", [P, HV, HD])
        den = sb("den", [P, H])
        rden = sb("rden", [P, H])
        attn = sb("attn", [P, D])
        yT = sb("yT", [P, KC, TP])

        mx = sb("mx", [P, TILES])
        score = sb("score", [P, TILES, E])
        sums = sb("sums", [P, TILES])
        thr = sb("thr", [P, 3, E], I32)
        cand = sb("cand", [P, E], I32)
        gain2 = sb("gain2", [P, E], I32)
        step3 = sb("step3", [P, 3, E], I32)
        next3 = sb("next3", [P, 3, E], I32)
        enough = sb("enough", [P, 3, E])
        cmp = sb("cmp", [P, TILES, 3, E], BF16)
        ge = sb("ge", [P, TILES, 2, E], BF16)
        gef = sb("gef", [P, 2, TILES, E])
        pos = sb("pos", [P, TILES, E])
        pos2 = sb("pos2", [P, TILES, E])
        pos_b = sb("pos_b", [P, TILES, E], BF16)
        iota_b = sb("iota_b", [P, HC], BF16)
        cgt = sb("cgt", [P, E])
        onehot = [sb(f"onehot{b}", [P, TILES, 2, HC], BF16) for b in range(2)]
        digits = sb("digits", [P, TILES, E, 4], BF16)
        slotf = sb("slotf", [HC, E, 4])
        warm = sb("warm", [1, 2])
        slot = sb("slot", [HC, E, 2], U32)
        gel_sh = sb("gel_sh", [P, 512])
        flat3 = lambda t: t[:].rearrange("p k n -> p (k n)")
        hshT = [flat3(wtok_s)[:, 0:TP], flat3(wqkv_s)[:, 0:TP], wex_s[1][:, WGU:WGU + TP], hsh_s[:]]
        as16 = lambda t: flat3(t).bitcast(F16)
        n16 = WGU // HALVES

        def w16(par, part, piece):
            if par == 0:
                return as16((wfc_s, wproj_s)[part])[:, piece * n16:(piece + 1) * n16]
            if part == 0:
                return as16(wsh_s)[:, piece * n16:(piece + 1) * n16]
            if piece < 6:
                return as16(wtok_s)[:, piece * n16:(piece + 1) * n16]
            return as16(wqkv_s)[:, (piece - 6) * n16:(piece - 5) * n16]

        slot_g = [sb(f"slot_g{b}_{k}", [HC, 1], U32) for b in range(2) for k in range(2)]
        slot_s = [sb(f"slot_s{b}_{k}", [HC, 1], U32) for b in range(2) for k in range(2)]
        weight = [sb(f"weight{b}_{k}", [HC, 1]) for b in range(2) for k in range(2)]
        xg = [sb(f"xg{b}_{k}", [HC, ROW]) for b in range(2) for k in range(2)]
        taken = 0

        def part(n):
            nonlocal taken
            taken += n
            assert taken <= SCRATCH
            return scratch[:, taken - n:taken]

        xgT = [part(KC * C).rearrange("p (k c) -> p k c", k=KC) for _ in range(2)]
        x16 = [[part(KC * C // 2).bitcast(F16).rearrange("p (k c) -> p k c", k=KC) for _ in range(2)] for _ in range(2)]
        gel = [part(2 * C) for _ in range(2)]
        hexT = part(MC * C).rearrange("p (m c) -> p m c", m=MC)
        eoT = part(KC * C).rearrange("p (k c) -> p k c", k=KC)
        eo = [part(D)[0:HC] for _ in range(4)]

        w_in = {n: sem(f"in_{n}") for n in ("bias", "consts", "tok", "qkv", "o", "fc", "proj", "moe")}
        patch_in = [sem(f"patch_in{b}") for b in range(2)]
        gu_in = [sem(f"gu_in{b}") for b in range(2)]
        dn_in = [sem(f"dn_in{b}") for b in range(2)]
        y_out = [sem(f"y_out{b}") for b in range(2)]
        score_out = sem("score_out")
        init_out = sem("init_out")
        ones_made, casts_made, bias_made = sem("ones_made"), sem("casts_made"), sem("bias_made")
        bias_out, bias_in = sem("bias_out"), sem("bias_in")
        tok_done, h_copied = sem("tok_done"), sem("h_copied")
        a_stats, a_shift, a_rstd, x0_made, xh_made = sem("a_stats"), sem("a_shift"), sem("a_rstd"), sem("x0_made"), sem("xh_made")
        xh_turned, xnT_made = sem("xh_turned"), sem("xnT_made")
        qk_done, v_done, neg_made, exp_made, v_made = sem("qk_done"), sem("v_done"), sem("neg_made"), sem("exp_made"), sem("v_made")
        qk_made, attn_made = sem("qk_made"), sem("attn_made")
        prod_made, num_done = sem("prod_made"), sem("num_done")
        attn_turned, attnT_made, o_done = sem("attn_turned"), sem("attnT_made"), sem("o_done")
        x1_made, c_stats, c_rstd, x2_made = sem("x1_made"), sem("c_stats"), sem("c_rstd"), sem("x2_made")
        x2_turned, x2T_made = sem("x2_turned"), sem("x2T_made")
        fc_done, hid_made = sem("fc_done"), sem("hid_made")
        proj_done, hx_made, h2_made = sem("proj_done"), sem("hx_made"), sem("h2_made")
        f_stats, f_rstd, y_made = sem("f_stats"), sem("f_rstd"), sem("y_made")
        y_turned, yT_made = sem("y_turned"), sem("yT_made")
        v_passed, a_passed, p_passed = sem("v_passed"), sem("a_passed"), sem("p_passed")
        v_chain, p_chain = sem("v_chain"), sem("p_chain")
        logits_done, centred, exps_made, scores_made = sem("logits_done"), sem("centred"), sem("exps_made"), sem("scores_made")
        cmp_made, counted = sem("cmp_made"), sem("counted")
        split_made, prefixed = sem("split_made"), sem("prefixed")
        digits_made, hot_made, slots_done, slots_made = sem("digits_made"), sem("hot_made"), sem("slots_done"), sem("slots_made")
        sgu_done, sgel_made, shid_made = sem("sgu_done"), sem("sgel_made"), sem("shid_made")
        sd_done, init_made = sem("sd_done"), sem("init_made")
        slot_copied = sem("slot_copied")
        row_in = [sem(f"row_in{b}") for b in range(2)]
        whi_made, wlo_made = sem("whi_made"), sem("wlo_made")
        xhi_made, xlo_made = sem("xhi_made"), sem("xlo_made")
        x_turned, xgT_made = sem("x_turned"), sem("xgT_made")
        egu_done, egel_made, ehid_made = sem("egu_done"), sem("egel_made"), sem("ehid_made")
        down_done, eoT_made, e_turned, eo_made = sem("down_done"), sem("eoT_made"), sem("e_turned"), sem("eo_made")
        scattered, weight_made = sem("scattered"), sem("weight_made")

        FOUND_LATE = 5
        BESIDE_PAIR = (range(0, 3), range(3, 6), range(6, 8), ())

        block = ctx.enter_context(nc.Block())

        SPAN = 2 * P
        width = lambda lo: min(SPAN, T - lo)
        rows_of = lambda t: min(P, T - t * P)
        SHARED = [(lo, m) for lo in range(0, TP, SPAN) for m in range(SC)]
        EARLY = 9
        REUSE = lambda j: 2 if j < EARLY + 2 else 4
        STEPS = 4 * (len(SHARED) - EARLY)
        BEFORE = 4
        QUOTA = 4
        BESIDE = [max(0, min(QUOTA, STEPS - BEFORE - r * QUOTA)) or QUOTA for r in range(ROUNDS)]
        HIDE = {r: [j for j in range(EARLY, len(SHARED)) if max(1, -(-(4 * (j - EARLY + 1) - BEFORE) // QUOTA)) == r]
                for r in range(ROUNDS)}

        @block.sync
        def _(sp):
            def load_patch(s):
                sp.dma_start(patch_s[s.par][:], patches[s.n]).then_inc(patch_in[s.par], 16)
                sp.dma_start(sel_s[s.par][:], sel[s.n]).then_inc(patch_in[s.par], 16)

            sp.dma_start(wtok_s[:], wtok).then_inc(w_in["tok"], 16)
            load_patch(Step(0, 0))
            sp.dma_start(base_s[:], base).then_inc(w_in["tok"], 16)
            sp.wait_ge(bias_made, 5)
            sp.dma_start(parts.rearrange("n (p j) -> p n j", p=P), bpart[:]).then_inc(bias_out, 16)
            load_patch(Step(0, 1))
            sp.wait_ge(ones_made, 1)
            sp.wait_ge(bias_out, 16)
            for n, q in enumerate(PARTS):
                sp.dma_start(bias_s[q:q + 1, :], parts[n:n + 1, :]).then_inc(bias_in, 16)
            sp.dma_start(wo_s[:], wo).then_inc(w_in["o"], 16)
            sp.dma_start(wfc_s[:], wfc).then_inc(w_in["fc"], 16)
            sp.dma_start(wproj_s[:], wproj).then_inc(w_in["proj"], 16)

            def load_gu(s, e):
                sp.dma_start(wex_s[s.par][:, 0:WGU], wex[e, :, 0:WGU]).then_inc(gu_in[s.par], 16)

            def load_dn(s, e):
                sp.dma_start(wex_s[s.par][:, WGU:WEX], wex[e, :, WGU:WEX]).then_inc(dn_in[s.par], 16)

            def store_y(s):
                sp.wait_ge(y_made, s.times(1, 1))
                sp.dma_start(rows[bass.ds(s.n * P, P), 0:D], y_s[s.par][:]).then_inc(y_out[s.par], 16)

            def next_patch(s):
                sp.wait_ge(tok_done, s.times(1, -1))
                load_patch(s)

            next_patch(Step(0, 2))
            sp.dma_start(gate_s[:], gate).then_inc(w_in["moe"], 16)
            sp.dma_start(wsh_s[:], wsh).then_inc(w_in["moe"], 16)
            sp.dma_start(wsd_s[:], wsd).then_inc(w_in["moe"], 16)
            next_patch(Step(0, 3))
            next_patch(Step(0, 4))
            load_gu(Step(0, 0), 0)
            load_dn(Step(0, 0), 0)
            load_gu(Step(0, 1), 1)
            with sp.Fori(0, 2) as i:
                for c in (1, 2):
                    next_patch(Step(i, c + 4))
                    store_y(Step(i, c - 1))
            next_patch(Step(0, TILES - 1))
            for t in range(4, TILES):
                store_y(Step(0, t))
            sp.wait_ge(scores_made, 1)
            sp.dma_start(rows[:, D:ROW].rearrange("(t p) e -> p t e", p=P), score[:]).then_inc(score_out, 16)
            sp.wait_ge(sd_done, TILES)
            load_dn(Step(0, 1), 1)
            for t in range(0, TILES, 2):
                sp.wait_ge(init_made, t + 2)
                sp.dma_start(out[t * P:(t + 2) * P, :].rearrange("(t p) d -> p t d", p=P), h_all[:, t:t + 2, :]).then_inc(init_out, 16)

            def next_gu(s):
                sp.wait_ge(wlo_made, s.times(HALVES, -HALVES))
                load_gu(s, s.n)

            def next_dn(s):
                sp.wait_ge(down_done, s.times(1, -1))
                load_dn(s, s.n)

            next_gu(Step(0, 2))
            with sp.Fori(0, E // 2 - 2) as i:
                for u in (2, 3):
                    next_gu(Step(i, u + 1))
                    next_dn(Step(i, u))
            next_gu(Step(0, E - 1))
            next_dn(Step(0, E - 2))
            next_dn(Step(0, E - 1))

        @block.gpsimd
        def _(gp):
            gp.memset(bias_s[:], 0.0)
            gp.memset(nhalf[:], -0.5)
            gp.memset(minus[:], -1.0)
            gp.memset(ones_b[:], 1.0)
            gp.memset(warm[:], 0.0).then_inc(ones_made, 1)
            gp.wait_ge(ones_made, 1)

            def inverse_root(k, var, base_count):
                gp.sem_inc(p_passed, 1)
                gp.tensor_scalar(tmp[:, k:k + 1], var, EPS, None, ALU.add).then_inc(p_chain, 1)
                gp.wait_ge(p_chain, base_count(1))
                return gp.tensor_tensor(rstd[:, k:k + 1], tmp[:, k:k + 1], nhalf[:], ALU.pow)

            def shift_of(k, at):
                gp.wait_ge(p_chain, at(2))
                gp.tensor_tensor(tmp[:, 6 + k:7 + k], rstd[:, k:k + 1], mv[:, k, 0:1], ALU.mult).then_inc(p_chain, 1)
                gp.wait_ge(p_chain, at(3))
                return gp.tensor_tensor(shift[:, k:k + 1], tmp[:, 6 + k:7 + k], minus[:], ALU.mult)

            def norm_c(s, at):
                gp.wait_ge(c_stats, s.times(1, 1))
                gp.wait_ge(x2_made, s.times(1, 0))
                inverse_root(1, mv[:, 1, 1:2], at).then_inc(p_chain, 1)
                shift_of(1, at).then_inc(c_rstd, 1)

            def norm_a(s, at):
                gp.wait_ge(a_stats, s.times(1, 1))
                gp.wait_ge(xh_made, s.times(1, 0))
                inverse_root(0, mv[:, 0, 1:2], at).then_inc(p_chain, 1)
                shift_of(0, at).then_inc(a_shift, 1)
                gp.tensor_tensor(tmp[:, 4:5], rstd[:, 0:1], rstd[:, 0:1], ALU.mult).then_inc(p_chain, 1)
                gp.wait_ge(p_chain, at(4))
                gp.tensor_tensor(tmp[:, 5:6], tmp[:, 4:5], mv[:, 0, 1:2], ALU.mult).then_inc(p_chain, 1)
                gp.wait_ge(p_chain, at(5))
                inverse_root(3, tmp[:, 5:6], lambda k: at(5 + k)).then_inc(a_rstd, 1)

            def norm_f(s, at):
                gp.wait_ge(f_stats, s.times(1, 1))
                gp.wait_ge(y_made, s.times(1, 0))
                inverse_root(2, mv[:, 2, 1:2], at).then_inc(p_chain, 1)
                shift_of(2, at).then_inc(f_rstd, 1)

            def sum_hx(s):
                gp.wait_ge(x1_made, s.times(1, 1))
                gp.wait_ge(h2_made, s.times(1, 0))
                gp.tensor_tensor(hx[:], h_all[:, s.n, :], x_all[:, s.n, :], ALU.add).then_inc(hx_made, 1)

            for t in range(3):
                norm_a(Step(0, t), lambda k, t=t: 6 * t + k)

            def turn(s):
                at = lambda k: s.times(12, 6 + k)
                norm_c(s.off(-1), at)
                sum_hx(s.off(-1))
                norm_a(s.off(2), lambda k: at(3 + k))
                norm_f(s.off(-1), lambda k: at(9 + k))

            with gp.Fori(0, 3) as i:
                turn(Step(i, 1))
                turn(Step(i, 2))
            turn(Step(0, 7))
            count = 6 + 12 * 8
            for c in (TILES - 2, TILES - 1, TILES):
                s = Step(0, c - 1)
                norm_c(s, lambda k: count + k)
                sum_hx(s)
                norm_f(s, lambda k: count + 3 + k)
                count += 6

            def gather(s, first):
                gp.wait_ge(slot_copied, s.times(2, 2))
                if not first:
                    gp.wait_ge(x_turned, s.times(1, -1))
                    gp.wait_ge(weight_made, s.times(2, -2))
                for k in range(2):
                    b = 2 * s.par + k
                    gp.sem_inc(p_passed, 1)
                    gp.indirect_dma_start(xg[b][:], None, rows, bass.IndirectOffsetOnAxis(slot_g[b][:], 0))\
                      .then_inc(row_in[s.par], 16)

            def scatter(s, k):
                b = 2 * s.par + k
                gp.wait_ge(eo_made, s.times(2, 1 + k))
                if not (isinstance(s.n, int) and s.n == 0):
                    gp.wait_ge(scattered, s.times(32, 0))
                gp.sem_inc(p_passed, 1)
                gp.indirect_dma_start(out, bass.IndirectOffsetOnAxis(slot_s[b][:], 0), eo[b], None,
                                      compute_op=ALU.add).then_inc(scattered, 16)

            def turn_rows(s, last):
                scatter(s.off(-1), 0)
                if not last:
                    gather(s.off(2), False)
                scatter(s.off(-1), 1)

            for b in range(2):
                gp.wait_ge(y_out[b], 16 * TILES // 2)
            gp.wait_ge(score_out, 16)
            gather(Step(0, 0), True)
            gather(Step(0, 1), True)
            gather(Step(0, 2), False)
            gp.wait_ge(init_out, 16 * TILES // 2)
            turn_rows(Step(0, 1), False)
            with gp.Fori(0, E // 2 - 2) as i:
                turn_rows(Step(i, 2), False)
                turn_rows(Step(i, 3), False)
            for e in (E - 2, E - 1, E):
                turn_rows(Step(0, e), True)
            gp.wait_ge(scattered, 32 * E)

        @block.scalar
        def _(act):
            def load_exp():
                act.activation(warm[:, 1:2], warm[:, 0:1], ACT.Exp)

            act.dma_start(braw[:], bias).then_inc(w_in["bias"], 16)
            act.dma_start(kst[:], consts).then_inc(w_in["consts"], 16)
            act.dma_start(colc[:], cols).then_inc(w_in["consts"], 16)
            act.dma_start(wqkv_s[:], wqkv).then_inc(w_in["qkv"], 16)
            act.wait_ge(ones_made, 1)
            load_exp()

            def copy_h(s):
                act.wait_ge(tok_done, s.times(1, 1))
                act.activation(h_all[:, s.n, :], ps_tok[:, 0:D], ACT.Copy).then_inc(h_copied, 1)

            def norm(dst, src, k, done):
                act.sem_inc(a_passed, 1)
                act.activation(dst, src, ACT.Identity, scale=rstd[:, k:k + 1], bias=shift[:, k:k + 1]).then_inc(done, 1)

            def norm_a(s):
                act.wait_ge(a_shift, s.times(1, 1))
                norm(x_all[:, s.n, :], h_all[:, s.n, :], 0, x0_made)

            def norm_c(s):
                act.wait_ge(c_rstd, s.times(1, 1))
                norm(x2[s.par][:], x_all[:, s.n, :], 1, x2_made)

            def norm_f(s, has_older=True):
                act.wait_ge(f_rstd, s.times(1, 1))
                if has_older:
                    act.wait_ge(y_out[s.par], s.half * 16)
                norm(y_s[s.par][:], h_all[:, s.n, :], 2, y_made)

            def scale_xh(s):
                act.wait_ge(a_rstd, s.times(1, 1))
                act.wait_ge(x0_made, s.times(1, 1))
                act.sem_inc(a_passed, 1)
                act.activation(xh[s.par][:], x_all[:, s.n, :], ACT.Copy, scale=rstd[:, 3:4]).then_inc(xh_made, 1)

            def affine(dst, src, w, b):
                for k in range(KC):
                    last = act.activation(dst[:, k, :], src[:, k * P:(k + 1) * P], ACT.Identity,
                                          scale=colc[:, w + k:w + k + 1], bias=colc[:, b + k:b + k + 1])
                return last

            def turn_xn(s):
                act.wait_ge(xh_turned, s.times(1, 1))
                affine(xnT, ps_xn, COL_LN1W, COL_LN1B).then_inc(xnT_made, 1)

            def negate_qk(s):
                act.wait_ge(qk_done, s.times(1, 1))
                act.wait_ge(qk_made, s.times(1, 0))
                act.activation(neg[:], ps_qk[:], ACT.Relu, scale=-1.0).then_inc(neg_made, 1)

            def exp_qk(s):
                act.wait_ge(neg_made, s.times(1, 1))
                act.activation(expo[:], neg[:], ACT.Exp, scale=-1.0).then_inc(exp_made, 1)

            def copy_v(s):
                act.wait_ge(v_done, s.times(1, 1))
                act.activation(vx[s.par][:].rearrange("p e h -> p (e h)"), ps_v[:, 0:D], ACT.Copy).then_inc(v_made, 1)

            def turn_attn(s):
                act.wait_ge(attn_turned, s.times(1, 1))
                act.activation(attnT[:].rearrange("p k t -> p (k t)"), ps_tr[:, 0:D], ACT.Copy).then_inc(attnT_made, 1)

            def turn_x2(s):
                act.wait_ge(x2_turned, s.times(1, 1))
                affine(x2T, ps_tr, COL_LN2W, COL_LN2B).then_inc(x2T_made, 1)

            def gelu(s):
                for g in range(2):
                    act.wait_ge(fc_done, s.times(2, g + 1))
                    for k in range(4):
                        m = 4 * g + k
                        last = act.activation(hidT[:, m, :], ps_fc[g][:, k * P:(k + 1) * P], ACT.Gelu,
                                              bias=colc[:, COL_FCB + m:COL_FCB + m + 1])
                    last.then_inc(hid_made, 1)

            def turn_y(s):
                act.wait_ge(y_turned, s.times(1, 1))
                act.activation(yT[:, :, bass.ds(s.n * P, P)], ps_y.rearrange("p (k t) -> p k t", k=KC),
                               ACT.Copy).then_inc(yT_made, 1)

            act.wait_ge(w_in["consts"], 32)
            copy_h(Step(0, 0))
            norm_a(Step(0, 0))
            scale_xh(Step(0, 0))
            copy_h(Step(0, 1))
            turn_xn(Step(0, 0))
            copy_v(Step(0, 0))
            negate_qk(Step(0, 0))
            exp_qk(Step(0, 0))
            norm_a(Step(0, 1))
            scale_xh(Step(0, 1))
            turn_xn(Step(0, 1))

            def gelu_shared(j):
                act.wait_ge(sgu_done, j + 1)
                if j >= 2:
                    act.wait_ge(shid_made, j - 1)
                n = width(SHARED[j][0])
                act.activation(gel_sh[:, (j % 2) * SPAN:(j % 2) * SPAN + n], ps_shared(j)[:, 0:n],
                               ACT.Gelu).then_inc(sgel_made, 1)

            def turn(s, older, prev, nxt, third, blocks=()):
                if nxt:
                    load_exp()
                if prev:
                    turn_attn(s.off(-1))
                if older:
                    norm_f(s.off(-2), not isinstance(s.n, int) or s.n >= 4)
                if nxt:
                    copy_v(s.off(1))
                    negate_qk(s.off(1))
                    exp_qk(s.off(1))
                if prev:
                    norm_c(s.off(-1))
                if older:
                    turn_y(s.off(-2))
                for j in blocks:
                    gelu_shared(j)
                if prev:
                    turn_x2(s.off(-1))
                if third:
                    copy_h(s.off(2))
                if prev:
                    gelu(s.off(-1))
                if third:
                    norm_a(s.off(2))
                    scale_xh(s.off(2))
                    turn_xn(s.off(2))

            turn(Step(0, 0), False, False, True, True)
            for c in (1, 2, 3):
                turn(Step(0, c), c > 1, True, True, True)
            with act.Fori(0, 2) as i:
                turn(Step(i, 4), True, True, True, True)
                turn(Step(i, 5), True, True, True, True)
            turn(Step(0, 8), True, True, True, False, (0,))
            s9 = Step(0, TILES - 1)
            s8 = s9.off(-1)
            turn_attn(s8)
            norm_f(s8.off(-1))
            norm_c(s8)
            gelu_shared(1)
            turn_y(s8.off(-1))
            gelu_shared(2)
            turn_x2(s8)
            gelu(s8)
            gelu_shared(3)
            gelu_shared(4)
            turn_attn(s9)
            norm_f(s8)
            norm_c(s9)
            turn_y(s8)
            gelu_shared(5)
            gelu_shared(6)
            turn_x2(s9)
            gelu_shared(7)
            gelu(s9)
            norm_f(s9)
            gelu_shared(8)
            load_exp()
            turn_y(s9)

            act.wait_ge(centred, 1)
            act.activation(score[:], score[:], ACT.Exp).then_inc(exps_made, 1)

            def split_w(s, pieces):
                for n in pieces:
                    if n == 0:
                        act.wait_ge(gu_in[s.par], s.half * 16 + 16)
                        act.sem_inc(a_passed, 1)
                    act.activation(w16(s.par, 0, n), wex_s[s.par][:, n * n16:(n + 1) * n16], ACT.Copy, scale=SPLIT).then_inc(whi_made, 1)

            act.wait_ge(proj_done, TILES)
            for j in range(EARLY, len(SHARED)):
                gelu_shared(j)
                if j - EARLY < HALVES:
                    split_w(Step(0, 0), (j - EARLY,))

            def turn_x(s):
                act.wait_ge(x_turned, s.times(1, 1))
                act.activation(xgT[s.par].rearrange("p k c -> p (k c)"), ps_xt[:, 0:KC * C],
                               ACT.Copy, scale=SPLIT).then_inc(xgT_made, 1)
                act.activation(x16[s.par][0].rearrange("p k c -> p (k c)"), ps_xt[:, 0:KC * C],
                               ACT.Copy, scale=SPLIT).then_inc(xhi_made, 1)

            def gelu_e(s, p):
                act.wait_ge(egu_done, s.times(PAIRS, p + 1))
                act.activation(gel[p % 2], ps_gate[p % 2][:, 0:2 * C], ACT.Gelu,
                               scale=1 / SPLIT ** 2).then_inc(egel_made, 1)

            def copy_eoT(s):
                act.wait_ge(down_done, s.times(1, 1))
                for k in range(KC):
                    last = act.activation(eoT[:, k, :], ps_down[k][:, 0:C], ACT.Copy)
                last.then_inc(eoT_made, 1)

            def expert(s, first, last):
                gelu_e(s, 0)
                if not first:
                    copy_eoT(s.off(-1))
                for p in range(PAIRS):
                    if p:
                        gelu_e(s, p)
                    if p == 2 and not last:
                        turn_x(s.off(1))
                    if not last:
                        split_w(s.off(1), BESIDE_PAIR[p])

            turn_x(Step(0, 0))
            expert(Step(0, 0), True, False)
            with act.Fori(0, E // 2 - 1) as i:
                expert(Step(i, 1), False, False)
                expert(Step(i, 2), False, False)
            expert(Step(0, E - 1), False, True)
            copy_eoT(Step(0, E - 1))

        @block.vector
        def _(ve):
            ve.wait_ge(w_in["bias"], 16)
            step = 0
            src = braw
            for n in range(len(PARTS)):
                ve.tensor_copy(bpart[:, n, :], src[:]).then_inc(bias_made, 1)
                step += 1
                if n < len(PARTS) - 1:
                    ve.wait_ge(bias_made, step)
                    ve.tensor_tensor(brest[:], src[:], bpart[:, n, :], ALU.subtract).then_inc(bias_made, 1)
                    step += 1
                    ve.wait_ge(bias_made, step)
                src = brest
            ve.wait_ge(w_in["consts"], 32)
            ve.tensor_copy(iota_b[:], kst[:, K_IOTA:K_IOTA + HC]).then_inc(v_passed, 1)
            ve.tensor_copy(tri_b[:], kst[:, K_TRI:K_TRI + P]).then_inc(casts_made, 1)

            def moments(k, src, at, done):
                ve.sem_inc(v_passed, 1)
                ve.bn_stats(stats[:, k, :], src).then_inc(v_chain, 1)
                ve.wait_ge(v_chain, at(1))
                ve.sem_inc(v_passed, 1)
                ve.bn_aggr(mv[:, k, :], stats[:, k, :]).then_inc(done, 1)

            def heads(ap, g):
                return ap.rearrange("p (h d) -> p h d", d=HD)[:, g * HH:(g + 1) * HH]

            def qk_product(s, g):
                q = heads(qk[s.par][:, 0:D], g).unsqueeze(2).to_broadcast([P, HH, H, HD])
                k = qk[s.par][:, D:2 * D].rearrange("p (j d) -> p j d", d=HD).unsqueeze(1).to_broadcast([P, HH, H, HD])
                ve.tensor_tensor(prod[g].rearrange("p (h j d) -> p h j d", h=HH, j=H), q, k, ALU.mult).then_inc(v_chain, 1)

            def qk_sum(s, g, at):
                ve.wait_ge(v_chain, at)
                ve.tensor_reduce(qkt[:, g * HH:(g + 1) * HH, :], prod[g].rearrange("p (h j d) -> p h j d", h=HH, j=H),
                                 AX, ALU.add).then_inc(v_chain, 1)

            def v_product_pe(s, at):
                n = H - HV
                ve.wait_ge(v_made, s.times(1, 1))
                ve.wait_ge(v_chain, at)
                a = qkt[:, HV:, :].rearrange("p h j -> p j h").unsqueeze(3).to_broadcast([P, H, n, HD])
                v = vx[s.par][:].rearrange("p e j -> p j e").unsqueeze(2).to_broadcast([P, H, n, HD])
                ve.tensor_tensor(prod_v[1].rearrange("p (j h e) -> p j h e", j=H, h=n), a, v, ALU.mult).then_inc(prod_made, 1)

            def v_product(s, at):
                ve.wait_ge(v_chain, at)
                a = qkt[:, 0:HV, :].unsqueeze(2).to_broadcast([P, HV, HD, H])
                v = vx[s.par][:].unsqueeze(1).to_broadcast([P, HV, HD, H])
                ve.tensor_tensor(prod_v[0].rearrange("p (h e j) -> p h e j", h=HV, e=HD), a, v, ALU.mult).then_inc(v_chain, 1)

            def v_sum(s, at):
                ve.wait_ge(v_chain, at)
                ve.tensor_reduce(num[:], prod_v[0].rearrange("p (h e j) -> p h e j", h=HV, e=HD), AX, ALU.add).then_inc(v_chain, 1)

            def divide(lo, n, src):
                out_h = attn[:].rearrange("p (h e) -> p h e", e=HD)[:, lo:lo + n]
                return ve.tensor_tensor(out_h, src, rden[:, lo:lo + n].unsqueeze(2).to_broadcast([P, n, HD]), ALU.mult)

            def a_moments(s, at):
                ve.wait_ge(h_copied, s.times(1, 1))
                ve.wait_ge(a_rstd, s.times(1, 0))
                moments(0, h_all[:, s.n, :], at, a_stats)

            def c_moments(s, at):
                ve.wait_ge(o_done, s.times(1, 1))
                ve.wait_ge(x0_made, s.times(1, 1))
                ve.tensor_tensor(x_all[:, s.n, :], ps_o[:, 0:D], x_all[:, s.n, :], ALU.add).then_inc(x1_made, 1)
                ve.wait_ge(x1_made, s.times(1, 1))
                ve.wait_ge(c_rstd, s.times(1, 0))
                moments(1, x_all[:, s.n, :], at, c_stats)

            def f_moments(s, at):
                ve.wait_ge(proj_done, s.times(1, 1))
                ve.wait_ge(hx_made, s.times(1, 1))
                ve.tensor_tensor(h_all[:, s.n, :], ps_proj[:, 0:D], hx[:], ALU.add).then_inc(h2_made, 1)
                ve.wait_ge(h2_made, s.times(1, 1))
                ve.wait_ge(f_rstd, s.times(1, 0))
                moments(2, h_all[:, s.n, :], at, f_stats)

            def combine(s):
                ve.wait_ge(exp_made, s.times(1, 1))
                ve.scalar_tensor_tensor(qk[s.par][:], ps_qk[:], 0.0, expo[:], ALU.max, ALU.add).then_inc(qk_made, 1)

            a_moments(Step(0, 0), lambda k: k)
            a_moments(Step(0, 1), lambda k: 1 + k)
            combine(Step(0, 0))
            CHAIN = 11

            def shared_hidden(j):
                lo, m = SHARED[j]
                ve.wait_ge(sgel_made, j + 1)
                n = width(lo)
                ve.tensor_tensor(hshT[m][:, lo:lo + n], ps_shared(j)[:, SPAN:SPAN + n],
                                 gel_sh[:, (j % 2) * SPAN:(j % 2) * SPAN + n], ALU.mult).then_inc(shid_made, 1)

            def turn(s, at, prev, nxt, third, blocks=()):
                n = 0

                def gain():
                    nonlocal n
                    n += 1
                    return at(n)

                ve.wait_ge(qk_made, s.times(1, 1))
                qk_product(s, 1)
                product1 = gain()
                if prev:
                    c_moments(s.off(-1), lambda k, n=n: at(n + k))
                    gain()
                qk_product(s, 0)
                product0 = gain()
                qk_sum(s, 1, product1)
                gain()
                qk_sum(s, 0, product0)
                sum0 = gain()
                v_product_pe(s, sum0)
                if third:
                    a_moments(s.off(2), lambda k, n=n: at(n + k))
                    gain()
                ve.wait_ge(v_chain, sum0)
                ve.tensor_reduce(den[:], qkt[:], AX, ALU.add).then_inc(v_chain, 1)
                summed = gain()
                if nxt:
                    combine(s.off(1))
                for j in blocks:
                    shared_hidden(j)
                v_product(s, sum0)
                product0 = gain()
                ve.wait_ge(v_chain, summed)
                ve.reciprocal(rden[:], den[:]).then_inc(v_chain, 1)
                gain()
                v_sum(s, product0)
                done = gain()
                ve.wait_ge(v_chain, done)
                divide(0, HV, num[:])
                ve.wait_ge(num_done, s.times(1, 1))
                divide(HV, H - HV, ps_num.rearrange("p (h e) -> p h e", e=HD)).then_inc(attn_made, 1)
                if prev:
                    f_moments(s.off(-1), lambda k, n=n: at(n + k))
                    gain()
                return n

            chain = 2
            chain += turn(Step(0, 0), lambda k: 2 + k, False, True, True)
            assert chain == CHAIN
            at = lambda s: lambda k: s.times(CHAIN, k)
            with ve.Fori(0, 3) as i:
                for c in (1, 2):
                    turn(Step(i, c), at(Step(i, c)), True, True, True)
            turn(Step(0, 7), at(Step(0, 7)), True, True, True)
            chain = CHAIN * 8
            chain += turn(Step(0, 8), lambda k: CHAIN * 8 + k, True, True, False, (0,))
            chain += turn(Step(0, 9), lambda k, c=chain: c + k, True, False, False, (1, 2))

            s9 = Step(0, TILES - 1)
            shared_hidden(3)
            shared_hidden(4)
            c_moments(s9, lambda k: chain + k)
            for j in (5, 6, 7):
                shared_hidden(j)
            f_moments(s9, lambda k: chain + 1 + k)
            shared_hidden(8)
            chain += 2

            def link(ins):
                nonlocal chain
                chain += 1
                ins.then_inc(v_chain, 1)
                ve.wait_ge(v_chain, chain)

            lg = ps_logit[:, 0:TILES * E].rearrange("p (t e) -> p t e", e=E)
            ve.wait_ge(logits_done, 1)
            link(ve.tensor_reduce(mx[:], lg, AX, ALU.max))
            ve.tensor_tensor(score[:], lg, mx[:].unsqueeze(2).to_broadcast([P, TILES, E]), ALU.subtract).then_inc(centred, 1)
            ve.wait_ge(exps_made, 1)
            link(ve.tensor_reduce(sums[:], score[:], AX, ALU.add))
            link(ve.reciprocal(sums[:], sums[:]))
            link(ve.tensor_tensor(score[:], score[:], sums[:].unsqueeze(2).to_broadcast([P, TILES, E]), ALU.mult))
            lim = kst[:, K_LIM:K_LIM + TILES * E].rearrange("p (t e) -> p t e", e=E)
            ve.tensor_tensor(score[:], score[:], lim, ALU.min).then_inc(scores_made, 1)
            ve.memset(cand[:], 0)
            for k in range(3):
                ve.memset(step3[:, k, :], (k + 1) << (BITS - 2))
                last = ve.memset(thr[:, k, :], (k + 1) << (BITS - 2))
            link(last)
            ve.wait_ge(scores_made, 1)

            def split_w(s, pieces):
                for n in pieces:
                    ve.wait_ge(whi_made, s.times(HALVES, n + 1))
                    ve.sem_inc(v_passed, 1)
                    ve.scalar_tensor_tensor(w16(s.par, 1, n), wex_s[s.par][:, n * n16:(n + 1) * n16], SPLIT, w16(s.par, 0, n),
                                            ALU.mult, ALU.subtract).then_inc(wlo_made, 1)

            def split_x(s):
                ve.wait_ge(xhi_made, s.times(1, 1))
                ve.tensor_tensor(x16[s.par][1], xgT[s.par], x16[s.par][0], ALU.subtract).then_inc(xlo_made, 1)

            def shared_out(t):
                ve.wait_ge(sd_done, (t | 1) + 1)
                n = rows_of(t)
                ve.tensor_tensor(h_all[0:n, t, :], ps_sd[t % 8][0:n], h_all[0:n, t, :], ALU.add).then_inc(init_made, 1)

            for r in range(ROUNDS):
                bit = BITS - 2 * r - 2
                ve.tensor_tensor(cmp[:], score[:].unsqueeze(2).to_broadcast([P, TILES, 3, E]),
                                 thr[:].bitcast(F32).unsqueeze(1).to_broadcast([P, TILES, 3, E]), ALU.is_ge).then_inc(cmp_made, 1)
                if r:
                    chain += 1
                    ve.tensor_tensor(cand[:], cand[:], gain2[:], ALU.bitwise_or).then_inc(v_chain, 1)
                if bit:
                    link(ve.tensor_scalar(step3[:], step3[:], 2, None, ALU.logical_shift_right))
                    chain += 1
                    ve.tensor_tensor(next3[:], step3[:], cand[:].unsqueeze(1).to_broadcast([P, 3, E]), ALU.bitwise_or)\
                      .then_inc(v_chain, 1)
                for j in HIDE[r]:
                    shared_hidden(j)
                if r >= ROUNDS - HALVES:
                    split_w(Step(0, 0), (r - (ROUNDS - HALVES),))
                ve.wait_ge(counted, r + 1)
                link(ve.tensor_scalar(enough[:].rearrange("p k e -> p (k e)"), ps_count[:, 0:3 * E], C - 0.5, float(1 << bit),
                                      ALU.is_ge, ALU.mult))
                with nc.allow_low_precision(reason="0 to 3 times a power of two: exact in float32, then cast to its integer"):
                    link(ve.tensor_reduce(gain2[:], enough[:].rearrange("p k e -> p e k"), AX, ALU.add))
                if bit:
                    link(ve.tensor_tensor(thr[:], next3[:], gain2[:].unsqueeze(1).to_broadcast([P, 3, E]), ALU.bitwise_or))
            link(ve.tensor_tensor(cand[:], cand[:], gain2[:], ALU.bitwise_or))

            tb = cand[:].bitcast(F32).unsqueeze(1).to_broadcast([P, TILES, E])
            for k, op in enumerate((ALU.is_gt, ALU.is_equal)):
                ve.tensor_tensor(ge[:, :, k, :], score[:], tb, op).then_inc(split_made, 1)
                ve.tensor_tensor(gef[:, k, :, :], score[:], tb, op)
            ve.wait_ge(prefixed, 1)
            pf = ps_prefix[:, 0:TILES * 2 * E].rearrange("p (t k e) -> p t k e", k=2, e=E)
            link(ve.tensor_copy(cgt[:], ps_count[:, 0:E]))
            link(ve.tensor_tensor(pos[:], pf[:, :, 1, :], cgt[:].unsqueeze(1).to_broadcast([P, TILES, E]), ALU.add))
            flat = lambda ap: ap.rearrange("p t e -> p (t e)")
            link(ve.scalar_tensor_tensor(flat(pos[:]), flat(pos[:]), -NOWHERE, flat(gef[:, 1]), ALU.add, ALU.mult))
            link(ve.tensor_scalar(pos2[:], pf[:, :, 0, :], -NOWHERE, None, ALU.add))
            link(ve.tensor_tensor(pos2[:], pos2[:], gef[:, 0], ALU.mult))
            link(ve.scalar_tensor_tensor(flat(pos[:]), flat(pos[:]), NOWHERE, flat(pos2[:]), ALU.add, ALU.add))
            link(ve.tensor_scalar(gef[:, 1], pos[:], float(HC) - 0.5, None, ALU.is_gt))
            link(ve.tensor_scalar(gef[:, 0], pos[:], float(HC) - 0.5, None, ALU.is_lt))
            for k, col in enumerate((K_CHUNK, K_PART)):
                v = kst[:, col:col + TILES * E].rearrange("p (t e) -> p t e", e=E)
                for b in range(2):
                    last = ve.tensor_tensor(digits[:, :, :, 2 * k + b], gef[:, b], v, ALU.mult)
            last.then_inc(digits_made, 1)
            link(ve.scalar_tensor_tensor(flat(pos_b[:]), flat(gef[:, 1]), -float(HC), flat(pos[:]), ALU.mult, ALU.add))
            iota = iota_b[:].unsqueeze(1).unsqueeze(1).to_broadcast([P, TILES, 2, HC])

            def hot(q):
                if q >= 2:
                    ve.wait_ge(slots_done, q - 1)
                a = pos_b[:, :, 2 * q:2 * q + 2].unsqueeze(3).to_broadcast([P, TILES, 2, HC])
                ve.tensor_tensor(onehot[q % 2][:], a, iota, ALU.is_equal).then_inc(hot_made, 1)

            def tokens(q):
                ve.wait_ge(slots_done, q + 1)
                f = slotf[:, 2 * q:2 * q + 2, :]
                ve.tensor_copy(f.rearrange("p e k -> p (e k)"), ps_slot[0:HC, 8 * q:8 * q + 8]).then_inc(slots_made, 1)
                ve.wait_ge(slots_made, q + 1)
                link(ve.scalar_tensor_tensor(slot[:, 2 * q:2 * q + 2, :], f[:, :, 0:2], float(P), f[:, :, 2:4], ALU.mult, ALU.add))

            def copy_slot(s):
                for k in range(2):
                    ve.tensor_copy(slot_g[2 * s.par + k][:], slot[:, s.n, k:k + 1]).then_inc(slot_copied, 1)

            hot(0)
            hot(1)
            tokens(0)
            copy_slot(Step(0, 0))
            copy_slot(Step(0, 1))
            shared_out(0)
            shared_out(1)
            hot(2)
            tokens(1)
            for t in range(2, 6):
                shared_out(t)
            tokens(2)
            shared_out(6)
            shared_out(7)
            split_x(Step(0, 0))
            shared_out(8)
            shared_out(9)
            hot(E // 2 - FOUND_LATE)

            def hidden(s, p):
                ve.wait_ge(egel_made, s.times(PAIRS, p + 1))
                ve.scalar_tensor_tensor(hexT[:, 2 * p:2 * p + 2, :].rearrange("p m c -> p (m c)"), ps_up[p % 2][:, 0:2 * C],
                                        1 / SPLIT ** 2, gel[p % 2], ALU.mult, ALU.mult).then_inc(ehid_made, 1)

            def take_weight(s):
                if not (isinstance(s.n, int) and s.n < 2):
                    ve.wait_ge(eo_made, s.times(2, -2))
                ve.wait_ge(row_in[s.par], s.half * 32 + 32)
                for k in range(2):
                    ve.tensor_copy(weight[2 * s.par + k][:], xg[2 * s.par + k][:, bass.ds(s.n + D, 1)]).then_inc(weight_made, 1)

            def weigh(s):
                if not (isinstance(s.n, int) and s.n < 2):
                    ve.wait_ge(scattered, s.times(32, -32))
                for k in range(2):
                    ve.tensor_copy(slot_s[2 * s.par + k][:], slot[:, s.n, k:k + 1])
                ve.wait_ge(e_turned, s.times(1, 1))
                ve.wait_ge(weight_made, s.times(2, 2))
                for k in range(2):
                    ve.tensor_scalar(eo[2 * s.par + k], ps_ot[0:HC, k * D:(k + 1) * D],
                                     weight[2 * s.par + k][:], None, ALU.mult).then_inc(eo_made, 1)

            def expert(s, first, last, q=None):
                nxt = not isinstance(s.n, int) or s.n < E - 1
                take_weight(s)
                if not last:
                    copy_slot(s.off(2))
                for p in range(PAIRS):
                    hidden(s, p)
                    if p == 1 and not first:
                        weigh(s.off(-1))
                    if p == 2 and nxt:
                        split_x(s.off(1))
                    if nxt:
                        split_w(s.off(1), BESIDE_PAIR[p])
                    if p == 0 and q is not None:
                        tokens(q)
                    if p == PAIRS - 1 and q is not None and q < E // 2 - 1:
                        hot(q + 1)

            for e in range(FOUND_LATE):
                expert(Step(0, e), e == 0, False, E // 2 - FOUND_LATE + e)
            with ve.Fori(0, (E - 3 - FOUND_LATE) // 2) as i:
                expert(Step(i, FOUND_LATE), False, False)
                expert(Step(i, FOUND_LATE + 1), False, False)
            expert(Step(0, E - 3), False, False)
            expert(Step(0, E - 2), False, True)
            expert(Step(0, E - 1), False, True)
            weigh(Step(0, E - 1))

        @block.tensor
        def _(pe):
            def turn_two(dst, src, done):
                for k in range(KC):
                    last = pe.transpose(dst[:, k * P:(k + 1) * P], src[:, k * P:(k + 1) * P], ident)
                last.then_inc(done, 1)

            def add_bias(dst, lo, n):
                pe.matmul(dst[:, 0:n], ones_b[0:BP, :], bias_s[:, lo:lo + n], start=True, stop=False)

            def embed(s, part=None):
                cut = TKC // 2
                if part != 1:
                    pe.wait_ge(patch_in[s.par], s.half * 32 + 32)
                    if not (isinstance(s.n, int) and s.n == 0):
                        pe.wait_ge(h_copied, s.times(1, 0))
                    pe.matmul(ps_tok[:, 0:D], sel_s[s.par][:], base_s[:], start=True, stop=False)
                for k in range(cut if part == 1 else 0, cut if part == 0 else TKC):
                    last = pe.matmul(ps_tok[:, 0:D], patch_s[s.par][:, k, :], wtok_s[:, k, :], start=False, stop=(k == TKC - 1))
                if part != 0:
                    last.then_inc(tok_done, 1)

            def turn_xh(s):
                pe.wait_ge(xh_made, s.times(1, 1))
                if not (isinstance(s.n, int) and s.n == 0):
                    pe.wait_ge(v_made, s.times(1, 0))
                turn_two(ps_xn, xh[s.par], xh_turned)

            def project_qk(s):
                if not (isinstance(s.n, int) and s.n == 0):
                    pe.wait_ge(qk_made, s.times(1, 0))
                add_bias(ps_qk, B_QKV, 2 * D)
                for k in range(KC):
                    last = pe.matmul(ps_qk[:], xnT[:, k, :], wqkv_s[:, k, 0:2 * D], start=False, stop=(k == KC - 1))
                last.then_inc(qk_done, 1)

            def project_v(s):
                pe.wait_ge(xnT_made, s.times(1, 1))
                add_bias(ps_v, B_QKV + 2 * D, D)
                for k in range(KC):
                    last = pe.matmul(ps_v[:, 0:D], xnT[:, k, :], wqkv_s[:, k, 2 * D:3 * D], start=False, stop=(k == KC - 1))
                last.then_inc(v_done, 1)

            def turn_attn(s):
                pe.wait_ge(attn_made, s.times(1, 1))
                turn_two(ps_tr, attn, attn_turned)

            def project_attn(s):
                pe.wait_ge(attnT_made, s.times(1, 1))
                if not (isinstance(s.n, int) and s.n == 0):
                    pe.wait_ge(x1_made, s.times(1, 0))
                add_bias(ps_o, B_O, D)
                for k in range(KC):
                    last = pe.matmul(ps_o[:, 0:D], attnT[:, k, :], wo_s[:, k, :], start=False, stop=(k == KC - 1))
                last.then_inc(o_done, 1)

            def turn_x2(s):
                pe.wait_ge(x2_made, s.times(1, 1))
                turn_two(ps_tr, x2[s.par], x2_turned)

            def mlp(s):
                pe.wait_ge(x2T_made, s.times(1, 1))
                for m in range(MC):
                    for k in range(KC):
                        last = pe.matmul(ps_fc[m // 4][:, (m % 4) * P:(m % 4 + 1) * P], wfc_s[:, k, m * P:(m + 1) * P],
                                         x2T[:, k, :], start=(k == 0), stop=(k == KC - 1))
                    if m % 4 == 3:
                        last.then_inc(fc_done, 1)

            def project_mlp(s):
                if not (isinstance(s.n, int) and s.n == 0):
                    pe.wait_ge(h2_made, s.times(1, 0))
                    pe.wait_ge(yT_made, s.times(1, 0))
                add_bias(ps_proj, B_PROJ, D)
                for m in range(MC):
                    if m % 4 == 0:
                        pe.wait_ge(hid_made, s.times(2, m // 4 + 1))
                    last = pe.matmul(ps_proj[:, 0:D], hidT[:, m, :], wproj_s[:, m, :], start=False, stop=(m == MC - 1))
                last.then_inc(proj_done, 1)

            def turn_y(s):
                pe.wait_ge(y_made, s.times(1, 1))
                turn_two(ps_y, y_s[s.par], y_turned)

            def sum_values(s):
                pe.wait_ge(prod_made, s.times(1, 1))
                pe.wait_ge(h_copied, TILES if isinstance(s.n, int) and s.n > TILES - 3 else s.times(1, 3))
                n = (H - HV) * HD
                for j in range(H):
                    last = pe.matmul(ps_num, ident, prod_v[1][:, j * n:(j + 1) * n], start=(j == 0), stop=(j == H - 1))
                last.then_inc(num_done, 1)

            def shared_gate_up(j):
                lo, m = SHARED[j]
                if j == 0:
                    pe.wait_ge(v_made, TILES)
                if j >= REUSE(j):
                    pe.wait_ge(shid_made, j - REUSE(j) + 1)
                for x in range(2):
                    for k in range(KC):
                        last = pe.matmul(ps_shared(j)[:, x * SPAN:x * SPAN + width(lo)],
                                         wsh_s[:, k, x * SH + m * P:x * SH + (m + 1) * P], yT[:, k, lo:lo + width(lo)],
                                         start=(k == 0), stop=(k == KC - 1))
                        if x == 1 and k == KC - 1:
                            last.then_inc(sgu_done, 1)
                        yield

            def logits(t):
                for k in range(KC):
                    last = pe.matmul(ps_logit[:, t * E:(t + 1) * E], yT[:, k, t * P:(t + 1) * P], gate_s[:, k, :],
                                     start=(k == 0), stop=(k == KC - 1))
                return last

            def early(*blocks):
                for j in blocks:
                    for _ in shared_gate_up(j):
                        pass

            def keep_busy(n):
                for _ in range(n):
                    pe.matmul(ps_tr[:], ones_b[:], ones_b[:].unsqueeze(1).to_broadcast([P, 4, P]), start=True, stop=True)

            pe.wait_ge(ones_made, 1)
            keep_busy(WARM)
            pe.wait_ge(w_in["tok"], 32)
            embed(Step(0, 0))
            embed(Step(0, 1))
            pe.wait_ge(w_in["consts"], 32)
            keep_busy(4)
            turn_xh(Step(0, 0))
            keep_busy(4)
            pe.wait_ge(bias_in, 16 * len(PARTS))
            pe.wait_ge(w_in["qkv"], 16)
            project_v(Step(0, 0))
            project_qk(Step(0, 0))
            keep_busy(10)
            turn_xh(Step(0, 1))
            keep_busy(4)

            def turn(s, older, prev, nxt, third, blocks=()):
                if prev:
                    turn_attn(s.off(-1))
                if nxt:
                    project_v(s.off(1))
                if prev:
                    project_attn(s.off(-1))
                if nxt:
                    project_qk(s.off(1))
                if third:
                    embed(s.off(2), 0)
                if older:
                    turn_y(s.off(-2))
                early(*blocks)
                if prev:
                    turn_x2(s.off(-1))
                if third:
                    embed(s.off(2), 1)
                if prev:
                    mlp(s.off(-1))
                    project_mlp(s.off(-1))
                sum_values(s)
                if third:
                    turn_xh(s.off(2))

            turn(Step(0, 0), False, False, True, True)
            pe.wait_ge(w_in["o"], 16)
            pe.wait_ge(w_in["fc"], 16)
            pe.wait_ge(w_in["proj"], 16)
            turn(Step(0, 1), False, True, True, True)
            with pe.Fori(0, 3) as i:
                turn(Step(i, 2), True, True, True, True)
                turn(Step(i, 3), True, True, True, True)
            pe.wait_ge(w_in["moe"], 48)
            turn(Step(0, 8), True, True, True, False, (0,))
            s9 = Step(0, TILES - 1)
            s8 = s9.off(-1)
            turn_attn(s8)
            project_attn(s8)
            early(1, 2)
            turn_y(s8.off(-1))
            turn_x2(s8)
            mlp(s8)
            project_mlp(s8)
            sum_values(s9)
            early(3, 4)

            turn_attn(s9)
            project_attn(s9)
            turn_y(s8)
            early(5, 6)
            turn_x2(s9)
            early(7)
            mlp(s9)
            project_mlp(s9)
            early(8)
            for t in range(TILES - 1):
                logits(t)
            turn_y(s9)
            pe.wait_ge(yT_made, TILES)
            logits(TILES - 1).then_inc(logits_done, 1)

            def shared_down(t):
                if t == 0:
                    pe.wait_ge(shid_made, len(SHARED))
                if t >= 8:
                    pe.wait_ge(init_made, 2)
                for m in range(SC):
                    last = pe.matmul(ps_sd[t % 8][0:rows_of(t)], hshT[m][:, t * P:t * P + rows_of(t)], wsd_s[:, m, :],
                                     start=(m == 0), stop=(m == SC - 1))
                    if m == SC - 1:
                        last.then_inc(sd_done, 1)
                    yield

            def chain_of(parts):
                for part in parts:
                    yield from part

            filler = chain_of([shared_gate_up(j) for j in range(EARLY, len(SHARED))] + [shared_down(t) for t in range(TILES)])

            def fill(n):
                for _ in range(n):
                    next(filler, None)

            fill(BEFORE)
            for r in range(ROUNDS):
                pe.wait_ge(cmp_made, r + 1)
                for t in range(TILES):
                    last = pe.matmul(ps_count[:, 0:3 * E], ones_b[:], cmp[:, t].rearrange("p k e -> p (k e)"),
                                     start=(t == 0), stop=(t == TILES - 1))
                last.then_inc(counted, 1)
                fill(BESIDE[r])
            pe.wait_ge(split_made, 2)
            pe.wait_ge(casts_made, 1)
            n = 2 * E
            g = ge[:].rearrange("p t k e -> p (t k e)")
            pe.matmul(ps_prefix[:, 0:TILES * n], tri_b[:], g, start=True, stop=False)
            for t in range(TILES - 1):
                left = TILES - 1 - t
                pe.matmul(ps_prefix[:, (t + 1) * n:TILES * n].rearrange("p (t c) -> p t c", c=n), ones_b[:],
                          g[:, t * n:(t + 1) * n].unsqueeze(1).to_broadcast([P, left, n]),
                          start=False, stop=(t == TILES - 2))
            for t in range(TILES):
                last = pe.matmul(ps_count[:, 0:E], ones_b[:], ge[:, t, 0, :], start=(t == 0), stop=(t == TILES - 1))
            last.then_inc(prefixed, 1)

            def slots(q):
                pe.wait_ge(hot_made, q + 1)
                if q:
                    pe.wait_ge(slots_made, q)
                for e in (2 * q, 2 * q + 1):
                    for t in range(TILES):
                        last = pe.matmul(ps_slot[0:HC, 4 * e:4 * e + 4], onehot[q % 2][:, t, e % 2, :], digits[:, t, e, :],
                                         start=(t == 0), stop=(t == TILES - 1))
                last.then_inc(slots_done, 1)

            left = STEPS + 4 * TILES - BEFORE - sum(BESIDE)
            assert left >= 12
            fill(left - 12)
            pe.wait_ge(digits_made, 1)
            slots(0)
            fill(4)
            slots(1)
            fill(4)
            slots(2)

            def turn_x(s):
                pe.wait_ge(row_in[s.par], s.half * 32 + 32)
                for b in range(2):
                    for k in range(KC):
                        last = pe.transpose(ps_xt[:, k * C + b * HC:k * C + (b + 1) * HC],
                                            xg[2 * s.par + b][:, k * P:(k + 1) * P], ident[0:HC, 0:HC])
                last.then_inc(x_turned, 1)

            pe.wait_ge(slots_made, E // 2 - FOUND_LATE)
            turn_x(Step(0, 0))
            fill(4)

            def gate_up(s, p):
                if p == 0:
                    pe.wait_ge(wlo_made, s.times(HALVES, HALVES))
                    pe.wait_ge(xlo_made, s.times(1, 1))
                if not (isinstance(s.n, int) and s.n == 0 and p < 2):
                    pe.wait_ge(ehid_made, s.times(PAIRS, p - 1))
                for w, dst in ((0, ps_gate), (KC, ps_up)):
                    for x in range(2):
                        m = 2 * p + x
                        products = [(k, a, b) for k in range(KC) for a, b in ((0, 0), (0, 1), (1, 0))]
                        for n, (k, a, b) in enumerate(products):
                            piece, lo = divmod((w + k) * MLP + m * P, n16)
                            last = pe.matmul(dst[p % 2][:, x * C:(x + 1) * C], w16(s.par, a, piece)[:, lo:lo + P],
                                             x16[s.par][b][:, k, :], start=(n == 0), stop=(n == len(products) - 1))
                last.then_inc(egu_done, 1)

            def down(s, p):
                if p == 0:
                    pe.wait_ge(dn_in[s.par], s.half * 16 + 16)
                pe.wait_ge(ehid_made, s.times(PAIRS, p + 1))
                for m in (2 * p, 2 * p + 1):
                    for k in range(KC):
                        lo = WGU + m * D + k * P
                        last = pe.matmul(ps_down[k][:, 0:C], wex_s[s.par][:, lo:lo + P], hexT[:, m, :],
                                         start=(m == 0), stop=(m == MC - 1))
                if p == PAIRS - 1:
                    last.then_inc(down_done, 1)

            def turn_eo(s):
                pe.wait_ge(eoT_made, s.times(1, 1))
                if not (isinstance(s.n, int) and s.n == 0):
                    pe.wait_ge(eo_made, s.times(2, 0))
                for b in range(2):
                    for k in range(KC):
                        last = pe.transpose(ps_ot[0:HC, b * D + k * P:b * D + (k + 1) * P], eoT[:, k, b * HC:(b + 1) * HC], ident)
                last.then_inc(e_turned, 1)

            def expert(s, first, last, q=None):
                gate_up(s, 0)
                if first:
                    pe.wait_ge(init_made, TILES)
                else:
                    down(s.off(-1), PAIRS - 1)
                gate_up(s, 1)
                if not first:
                    turn_eo(s.off(-1))
                if q is not None:
                    pe.wait_ge(xhi_made, s.times(1, 1))
                    slots(q)
                down(s, 0)
                gate_up(s, 2)
                if not last:
                    if q is not None:
                        pe.wait_ge(slots_made, q + 1)
                    turn_x(s.off(1))
                down(s, 1)
                gate_up(s, 3)
                down(s, 2)

            for e in range(FOUND_LATE):
                expert(Step(0, e), e == 0, False, E // 2 - FOUND_LATE + e)
            pe.wait_ge(slots_made, E // 2)
            with pe.Fori(0, (E - 1 - FOUND_LATE) // 2) as i:
                expert(Step(i, FOUND_LATE), False, False)
                expert(Step(i, FOUND_LATE + 1), False, False)
            expert(Step(0, E - 1), False, True)
            down(Step(0, E - 1), PAIRS - 1)
            turn_eo(Step(0, E - 1))


def _lay_out(inp):
    f = {k: np.asarray(v) for k, v in inp.items()}

    def chunks(w):
        return np.ascontiguousarray(w.T.reshape(-1, P, w.shape[0]).transpose(1, 0, 2))

    x = f["x"].reshape(IMAGES, 3, 6, 16, 6, 16).transpose(0, 2, 4, 1, 3, 5).reshape(IMAGES, GRID, PATCH_K)
    tok = np.zeros((TP, PATCH_K), x.dtype)
    tok[:T].reshape(IMAGES, SEQ, PATCH_K)[:, 1:] = x
    a = {"patches": np.ascontiguousarray(tok.reshape(TILES, P, TKC, P).transpose(0, 3, 2, 1))}

    sel = np.zeros((BASE, TP), np.float32)
    t = np.arange(T)
    sel[t % SEQ, t] = 1
    sel[np.where(t % SEQ == 0, SEQ + 1, SEQ), t] = 1
    a["sel"] = np.ascontiguousarray(sel.reshape(BASE, TILES, P).transpose(1, 0, 2))
    a["wtok"] = chunks(f["L0_tok_W"])
    a["base"] = np.concatenate([f["L0_tok_pos_embedding"][0], f["L0_tok_b"][None], f["L0_tok_class_token"][0]])
    turned = np.arange(D).reshape(H, HD).T.reshape(-1)
    order = [np.arange(D), np.arange(D), turned]
    ws = [f["L0_attn_%s_w" % n][o] for n, o in zip("qkv", order)]
    bs = [f["L0_attn_%s_b" % n][o] for n, o in zip("qkv", order)]
    a["wqkv"] = chunks(np.concatenate(ws))
    a["bias"] = np.concatenate(bs + [f["L0_attn_o_b"], f["L0_attn_proj_b"]]).reshape(P, -1)
    a["wo"] = chunks(f["L0_attn_o_w"])
    a["wfc"] = chunks(f["L0_attn_fc_w"])
    a["wproj"] = chunks(f["L0_attn_proj_w"])
    two = lambda v: v.reshape(-1, P).T
    a["cols"] = np.concatenate([two(f["L0_attn_" + n]) for n in ("ln1_w", "ln1_b", "ln2_w", "ln2_b", "fc_b")], axis=1)
    a["gate"] = chunks(f["L0_ffn_gate_w"])
    a["wsh"] = chunks(np.concatenate([f["L0_ffn_Sg"], f["L0_ffn_Su"]]))
    a["wsd"] = chunks(f["L0_ffn_Sd"])

    def expert_chunks(w):
        e, o, k = w.shape
        return w.transpose(0, 2, 1).reshape(e, k // P, P, o).transpose(0, 2, 1, 3).reshape(e, P, -1)

    a["wex"] = np.concatenate([expert_chunks(f["L0_ffn_" + n]) for n in ("Wg", "Wu", "Wd")], axis=2)
    c = np.zeros((P, KCOLS), np.float32)
    c[:, K_ID:K_ID + P] = np.eye(P)
    c[:, K_TRI:K_TRI + P] = np.triu(np.ones((P, P)), 1)
    tt = np.repeat(np.arange(TILES), E)
    c[:, K_CHUNK:K_CHUNK + TILES * E] = tt
    c[:, K_PART:K_PART + TILES * E] = np.arange(P)[:, None]
    c[:, K_LIM:K_LIM + TILES * E] = np.where(tt * P + np.arange(P)[:, None] < T, 2.0, -1.0)
    c[:, K_IOTA:] = np.arange(HC)
    a["consts"] = c
    return {k: np.ascontiguousarray(v) for k, v in a.items()}


_ORDER = ["patches", "sel", "wtok", "base", "wqkv", "bias", "wo", "wfc", "wproj", "cols", "gate",
          "wsh", "wsd", "wex", "consts"]


def kernel(**inputs):
    import concourse.bacc as _bacc
    from concourse.bass_utils import run_bass_kernel_spmd as _run

    laid = _lay_out(inputs)
    nc = _bacc.Bacc("TRN2", target_bir_lowering=False, num_devices=1)
    args = [nc.dram_tensor(f"in_{n}", laid[n].shape, mybir.dt.from_np(laid[n].dtype), kind="ExternalInput").ap()
            for n in _ORDER]
    args.append(nc.dram_tensor("out_rows", (TP, D), F32, kind="ExternalOutput").ap())
    vit_tower(nc, *args)
    r = _run(nc, [{f"in_{n}": laid[n] for n in _ORDER}], core_ids=[0])
    return r.results[0]["out_rows"][:T].reshape(IMAGES, SEQ, D)
```
